# Optimizing a Trainium2 kernel written in Bass

```python
import numpy as np
import jax
import jax.numpy as jnp

def _softmax(x, axis=-1):
    return jax.nn.softmax(x, axis=axis)

def _gelu(x):
    return jax.nn.gelu(x, approximate=True)

def _silu(x):
    return jax.nn.silu(x)

def _sigmoid(x):
    return jax.nn.sigmoid(x)

def _layernorm(x, axis=-1, eps=1e-05):
    m = jnp.mean(x, axis=axis, keepdims=True)
    v = jnp.var(x, axis=axis, keepdims=True)
    return (x - m) / jnp.sqrt(v + eps)

def _scatter_add(tgt, idx, src, axis=0):
    return tgt.at[idx].add(src)

def _segment_sum(src, seg, n):
    return jax.ops.segment_sum(src, seg, n)
kernel_name = 'mk_audio_tower_d1_tok_audfeat1024_r4_edd173'

def setup_inputs(seed: int=0):
    np.random.seed(seed)
    _w = jnp.asarray

    def _rec_inputs():
        import jax
        import jax.numpy as jnp
        _rk = jax.random.key(seed)
        x = -0.000125008 + 0.999885 * jax.random.normal(jax.random.fold_in(_rk, 1), (128, 250, 256), jnp.float32)
        return x
    x = _rec_inputs()

    def _L0_tok_setup():
        import jax, jax.numpy as jnp
        import numpy as np
        B, S, C = (8, 1024, 256)
        key = jax.random.key(seed)
        k1, k2 = jax.random.split(key)
        x = jax.random.normal(k1, (B, S, C), dtype=jnp.float32)
        w = jax.random.normal(k2, (C, C), dtype=jnp.float32) * 0.02 + 2.0 * jnp.eye(C, dtype=jnp.float32)
        return {'x': x, 'w': w}
    _L0_tok_all = _L0_tok_setup()
    _L0_tok_in = {k: v for k, v in _L0_tok_all.items() if k in ('w',)}
    del _L0_tok_all

    def _L0_attn_setup():
        import jax, jax.numpy as jnp
        import numpy as np
        B, T, C, H = (2, 256, 256, 16)
        K = C // H
        A = 32
        D = 64
        EPS = 1e-05

        def _rwkv6_forward(x, time_maa_x, time_maa_wkvrg, tm_w1, tm_w2, time_decay, td_w1, td_w2, time_faaaa, Wr, Wk, Wv, Wg, Wo, ln_w, ln_b):
            Bb, Tt, Cc = x.shape
            sx = jnp.concatenate([jnp.zeros_like(x[:, :1]), x[:, :-1]], axis=1) - x
            xxx = x + sx * time_maa_x
            m = jnp.tanh(xxx @ tm_w1).reshape(Bb, Tt, 5, A)
            delta = jnp.einsum('btfa,fac->btfc', m, tm_w2)
            mix = time_maa_wkvrg[None, None] + delta
            xw, xk, xv, xr, xg = [x + sx * mix[:, :, i] for i in range(5)]
            r = xr @ Wr
            k = xk @ Wk
            v = xv @ Wv
            g = jax.nn.silu(xg @ Wg)
            ww = time_decay + jnp.tanh(xw @ td_w1) @ td_w2
            w = jnp.exp(-jnp.exp(ww))
            tm = lambda z: z.reshape(Bb, Tt, H, K).transpose(1, 0, 2, 3)
            r_, k_, v_, w_ = (tm(r), tm(k), tm(v), tm(w))
            u = time_faaaa

            def step(state, rkvw):
                r_t, k_t, v_t, w_t = rkvw
                a = k_t[..., :, None] * v_t[..., None, :]
                y = jnp.einsum('bhk,bhkv->bhv', r_t, state + u[None, :, :, None] * a)
                new_state = w_t[..., :, None] * state + a
                return (new_state, y)
            state0 = jnp.zeros((Bb, H, K, K), x.dtype)
            _, ys = jax.lax.scan(step, state0, (r_, k_, v_, w_))
            y = ys.transpose(1, 0, 2, 3)
            mu = y.mean(-1, keepdims=True)
            var = ((y - mu) ** 2).mean(-1, keepdims=True)
            yn = (y - mu) * jax.lax.rsqrt(var + EPS)
            yn = yn * ln_w.reshape(H, K) + ln_b.reshape(H, K)
            return yn.reshape(Bb, Tt, Cc) * g @ Wo
        key = jax.random.key(seed)
        ks = jax.random.split(key, 17)
        n = lambda k, s, sc=0.02: jax.random.normal(k, s, jnp.float32) * sc
        u01 = lambda k, s: jax.random.uniform(k, s, jnp.float32)
        return {'x': jax.random.normal(ks[0], (B, T, C), jnp.float32), 'time_maa_x': u01(ks[1], (C,)), 'time_maa_wkvrg': u01(ks[2], (5, C)), 'tm_w1': n(ks[3], (C, 5 * A)), 'tm_w2': n(ks[4], (5, A, C)), 'time_decay': n(ks[5], (C,), 1.0) - 4.0, 'td_w1': n(ks[6], (C, D)), 'td_w2': n(ks[7], (D, C)), 'time_faaaa': n(ks[8], (H, K), 0.5), 'Wr': n(ks[9], (C, C)), 'Wk': n(ks[10], (C, C)), 'Wv': n(ks[11], (C, C)), 'Wg': n(ks[12], (C, C)), 'Wo': n(ks[13], (C, C)), 'ln_w': jnp.ones((C,), jnp.float32), 'ln_b': jnp.zeros((C,), jnp.float32)}
    _L0_attn_all = _L0_attn_setup()
    _L0_attn_in = {k: v for k, v in _L0_attn_all.items() if k in ('time_maa_x', 'time_maa_wkvrg', 'tm_w1', 'tm_w2', 'time_decay', 'td_w1', 'td_w2', 'time_faaaa', 'Wr', 'Wk', 'Wv', 'Wg', 'Wo', 'ln_w', 'ln_b')}
    del _L0_attn_all

    def _L0_ffn_setup():
        import jax, jax.numpy as jnp
        import numpy as np
        S, B, D, E, C, FF = (512, 4, 256, 8, 512, 1024)
        N = S * B
        key = jax.random.key(seed)
        ks = jax.random.split(key, 7)
        return {'hidden_states': jax.random.normal(ks[0], (S, B, D), dtype=jnp.float32), 'combine_weights': jax.random.uniform(ks[1], (N, E), dtype=jnp.float32), 'top_idx': jax.random.randint(ks[2], (C, E), 0, N, dtype=jnp.int64), 'W1': jax.random.normal(ks[3], (E, D, FF), dtype=jnp.float32) * (1.0 / np.sqrt(D)), 'b1': jnp.zeros((E, FF), dtype=jnp.float32), 'W2': jax.random.normal(ks[4], (E, FF, D), dtype=jnp.float32) * (1.0 / np.sqrt(FF)), 'b2': jnp.zeros((E, D), dtype=jnp.float32)}
    _L0_ffn_all = _L0_ffn_setup()
    _L0_ffn_in = {k: v for k, v in _L0_ffn_all.items() if k in ('combine_weights', 'top_idx', 'W1', 'b1', 'W2', 'b2')}
    del _L0_ffn_all
    return {'x': x, 'L0_tok_w': _L0_tok_in['w'], 'L0_attn_time_maa_x': _L0_attn_in['time_maa_x'], 'L0_attn_time_maa_wkvrg': _L0_attn_in['time_maa_wkvrg'], 'L0_attn_tm_w1': _L0_attn_in['tm_w1'], 'L0_attn_tm_w2': _L0_attn_in['tm_w2'], 'L0_attn_time_decay': _L0_attn_in['time_decay'], 'L0_attn_td_w1': _L0_attn_in['td_w1'], 'L0_attn_td_w2': _L0_attn_in['td_w2'], 'L0_attn_time_faaaa': _L0_attn_in['time_faaaa'], 'L0_attn_Wr': _L0_attn_in['Wr'], 'L0_attn_Wk': _L0_attn_in['Wk'], 'L0_attn_Wv': _L0_attn_in['Wv'], 'L0_attn_Wg': _L0_attn_in['Wg'], 'L0_attn_Wo': _L0_attn_in['Wo'], 'L0_attn_ln_w': _L0_attn_in['ln_w'], 'L0_attn_ln_b': _L0_attn_in['ln_b'], 'L0_ffn_combine_weights': _L0_ffn_in['combine_weights'], 'L0_ffn_top_idx': _L0_ffn_in['top_idx'], 'L0_ffn_W1': _L0_ffn_in['W1'], 'L0_ffn_b1': _L0_ffn_in['b1'], 'L0_ffn_W2': _L0_ffn_in['W2'], 'L0_ffn_b2': _L0_ffn_in['b2']}

def reference(x, L0_tok_w, L0_attn_time_maa_x, L0_attn_time_maa_wkvrg, L0_attn_tm_w1, L0_attn_tm_w2, L0_attn_time_decay, L0_attn_td_w1, L0_attn_td_w2, L0_attn_time_faaaa, L0_attn_Wr, L0_attn_Wk, L0_attn_Wv, L0_attn_Wg, L0_attn_Wo, L0_attn_ln_w, L0_attn_ln_b, L0_ffn_combine_weights, L0_ffn_top_idx, L0_ffn_W1, L0_ffn_b1, L0_ffn_W2, L0_ffn_b2):
    import jax
    import jax.numpy as jnp

    def _L0_tok_ref(x, w):
        import jax, jax.numpy as jnp
        import numpy as np
        B, S, C = (8, 1024, 256)
        x1 = x[:, 0::2, :]
        x2 = x[:, 1::2, :]
        window = jnp.stack([x1, x2], axis=2)
        scores = jnp.einsum('bspc,cd->bspd', window, w)
        weights = jax.nn.softmax(scores, axis=2)
        return (weights * window).sum(axis=2)

    def _L0_attn_ref(x, time_maa_x, time_maa_wkvrg, tm_w1, tm_w2, time_decay, td_w1, td_w2, time_faaaa, Wr, Wk, Wv, Wg, Wo, ln_w, ln_b):
        import jax, jax.numpy as jnp
        import numpy as np
        B, T, C, H = (2, 256, 256, 16)
        K = C // H
        A = 32
        D = 64
        EPS = 1e-05

        def _rwkv6_forward(x, time_maa_x, time_maa_wkvrg, tm_w1, tm_w2, time_decay, td_w1, td_w2, time_faaaa, Wr, Wk, Wv, Wg, Wo, ln_w, ln_b):
            Bb, Tt, Cc = x.shape
            sx = jnp.concatenate([jnp.zeros_like(x[:, :1]), x[:, :-1]], axis=1) - x
            xxx = x + sx * time_maa_x
            m = jnp.tanh(xxx @ tm_w1).reshape(Bb, Tt, 5, A)
            delta = jnp.einsum('btfa,fac->btfc', m, tm_w2)
            mix = time_maa_wkvrg[None, None] + delta
            xw, xk, xv, xr, xg = [x + sx * mix[:, :, i] for i in range(5)]
            r = xr @ Wr
            k = xk @ Wk
            v = xv @ Wv
            g = jax.nn.silu(xg @ Wg)
            ww = time_decay + jnp.tanh(xw @ td_w1) @ td_w2
            w = jnp.exp(-jnp.exp(ww))
            tm = lambda z: z.reshape(Bb, Tt, H, K).transpose(1, 0, 2, 3)
            r_, k_, v_, w_ = (tm(r), tm(k), tm(v), tm(w))
            u = time_faaaa

            def step(state, rkvw):
                r_t, k_t, v_t, w_t = rkvw
                a = k_t[..., :, None] * v_t[..., None, :]
                y = jnp.einsum('bhk,bhkv->bhv', r_t, state + u[None, :, :, None] * a)
                new_state = w_t[..., :, None] * state + a
                return (new_state, y)
            state0 = jnp.zeros((Bb, H, K, K), x.dtype)
            _, ys = jax.lax.scan(step, state0, (r_, k_, v_, w_))
            y = ys.transpose(1, 0, 2, 3)
            mu = y.mean(-1, keepdims=True)
            var = ((y - mu) ** 2).mean(-1, keepdims=True)
            yn = (y - mu) * jax.lax.rsqrt(var + EPS)
            yn = yn * ln_w.reshape(H, K) + ln_b.reshape(H, K)
            return yn.reshape(Bb, Tt, Cc) * g @ Wo
        return _rwkv6_forward(x, time_maa_x, time_maa_wkvrg, tm_w1, tm_w2, time_decay, td_w1, td_w2, time_faaaa, Wr, Wk, Wv, Wg, Wo, ln_w, ln_b)

    def _L0_ffn_ref(hidden_states, combine_weights, top_idx, W1, b1, W2, b2):
        import jax, jax.numpy as jnp
        import numpy as np
        S, B, D, E, C, FF = (512, 4, 256, 8, 512, 1024)
        N = S * B
        s, b, d = hidden_states.shape
        x = hidden_states.reshape(-1, d)
        tok = top_idx.T
        gathered = x[tok]
        h = jax.nn.gelu(jnp.einsum('ecd,edf->ecf', gathered, W1) + b1[:, None, :])
        out_e = jnp.einsum('ecf,efd->ecd', h, W2) + b2[:, None, :]
        e_ids = jnp.arange(tok.shape[0])[:, None]
        w = combine_weights[tok, e_ids]
        weighted = (out_e * w[..., None]).reshape(-1, d)
        out = jnp.zeros_like(x).at[tok.reshape(-1)].add(weighted)
        return out.reshape(s, b, d)
    h = _L0_tok_ref(x, L0_tok_w)
    h = h + _L0_attn_ref(_layernorm(h, axis=-1), L0_attn_time_maa_x, L0_attn_time_maa_wkvrg, L0_attn_tm_w1, L0_attn_tm_w2, L0_attn_time_decay, L0_attn_td_w1, L0_attn_td_w2, L0_attn_time_faaaa, L0_attn_Wr, L0_attn_Wk, L0_attn_Wv, L0_attn_Wg, L0_attn_Wo, L0_attn_ln_w, L0_attn_ln_b)
    h = h + _L0_ffn_ref(_layernorm(h, axis=-1), L0_ffn_combine_weights, L0_ffn_top_idx, L0_ffn_W1, L0_ffn_b1, L0_ffn_W2, L0_ffn_b2)
    return h

_drawn_inputs = setup_inputs


def setup_inputs(seed=0):
    import zlib

    import numpy as np

    out = dict(_drawn_inputs(seed))
    spreads = {'L0_attn_ln_w': (1.0, 0.6),
     'L0_attn_ln_b': (0.0, 0.8),
     'L0_ffn_b1': (0.0, 0.357),
     'L0_ffn_b2': (0.0, 0.1)}
    factors = {'L0_attn_time_maa_x': 8.0,
     'L0_attn_tm_w1': 8.0,
     'L0_attn_tm_w2': 8.0,
     'L0_attn_time_decay': 3.361,
     'L0_attn_td_w1': 8.0,
     'L0_attn_td_w2': 8.0,
     'L0_attn_time_faaaa': 8.0}
    for name, (base, spread) in spreads.items():
        noise = np.random.default_rng([zlib.crc32(name.encode()), seed]).standard_normal(out[name].shape)
        drawn = base * np.exp(spread * noise) if base else spread * noise
        out[name] = jnp.asarray(drawn.astype(out[name].dtype))
    for name, factor in factors.items():
        out[name] = (out[name] * factor).astype(out[name].dtype)
    return out
```

```python
from contextlib import ExitStack

import concourse.bass as bass
from concourse import mybir

F32 = mybir.dt.float32
BF16 = mybir.dt.bfloat16
I32 = mybir.dt.int32
ALU = mybir.AluOpType
ACT = mybir.ActivationFunctionType
AX_X = mybir.AxisListType.X

P = 128
C = 256
NC = C // P
T = 125
B = 128
GB = 4
GT = GB * T
NG = B // GB
H, K = 16, 16
HC = H // NC
LORA = 32
NMIX = 5
DW = 64
UNITS = NC * K
RING = 4
assert UNITS % RING == 0
EPS = 1e-5
E, CAP, FF, NTOK = 8, 512, 1024, 2048
NF = FF // P
TPE = CAP // P
NT = E * TPE
TABLE = NTOK + P

COL = {"maa_x": 0, "maa": NC, "decay": NC * 6, "u": NC * 7, "ln_w": NC * 8, "ln_b": NC * 9}
NPAR = NC * 10

FRONT_USES = (["tok0", "tok1", "mean", "var", "m", "m4"]
              + [f"delta{f}{c}" for f in range(NMIX) for c in range(NC)]
              + ["td", "ww0", "ww1", "k0", "k1", "v0", "v1", "r0", "r1", "g0", "g1",
                 "ruk", "vrow0", "vrow1"])
FRONT_INDEX = {name: k for k, name in enumerate(FRONT_USES)}
FRONT_BANKS = 3
FRONT_TURNS = len(FRONT_USES) // FRONT_BANKS
assert len(FRONT_USES) % FRONT_BANKS == 0
TAIL_USES = ["yT0", "yT1", "rows0", "rows1"]


def wait(eng, sem, value):
    if isinstance(value, int) and value <= 0:
        return
    eng.wait_ge(sem, value)


def walk(eng, slot):
    def one(scan, front, tail):
        for u in range(UNITS):
            slot(u, scan, front, tail)

    def at(g):
        return (g, g % 2, g // 2) if 0 <= g < NG else None

    one(None, at(0), None)
    one(at(0), at(1), None)
    one(at(1), at(2), at(0))
    with eng.Fori(1, NG // 2 - 1) as i:
        one((i * 2, 0, i), (i * 2 + 1, 1, i), (i * 2 - 1, 1, i - 1))
        one((i * 2 + 1, 1, i), (i * 2 + 2, 0, i + 1), (i * 2, 0, i))
    for g in range(NG - 2, NG + 1):
        one(at(g), at(g + 1), at(g - 1))


def attention_phase(nc, d, const):
    ident, params, ready = const
    with ExitStack() as ctx:
        def sb(name, shape, dt=F32):
            return ctx.enter_context(nc.sbuf_tensor(name, shape, dt))

        def ps(name, shape):
            return ctx.enter_context(nc.psum_tensor(name, shape, F32))

        def sem(name):
            return ctx.enter_context(nc.semaphore(name))

        w_tok = sb("w_tok", [P, NC, C])
        w_r = sb("w_r", [P, NC, C])
        w_k = sb("w_k", [P, NC, C])
        w_v = sb("w_v", [P, NC, C])
        w_g = sb("w_g", [P, NC, C])
        w_o = sb("w_o", [P, NC, C])
        tm_w1 = sb("tm_w1", [P, NC, NMIX * LORA])
        tm_w2 = sb("tm_w2", [P, C])
        tm_w2_last = sb("tm_w2_last", [LORA, C])
        td_w1 = sb("td_w1", [P, NC, DW])
        td_w2 = sb("td_w2", [DW, C])
        head_sel = sb("head_sel", [P, HC])
        head_u = sb("head_u", [P, NC, HC])
        value_sel = sb("value_sel", [P, K, P], BF16)
        mean_w = sb("mean_w", [P, P])
        neg_half = sb("neg_half", [P, 1])
        eps4 = sb("eps4", [P, 1])
        eps1 = sb("eps1", [P, 1])
        half_ln = sb("half_ln", [P, 2 * NC])

        x_in = sb("x_in", [P, 2, 2 * NC, GT])
        diff = sb("diff", [P, NC, GT])
        summ = sb("summ", [P, NC, GT])
        th_sq = sb("th_sq", [P, GB * C])
        th = th_sq[:, 0:NC * GT].rearrange("p (c n) -> p c n", c=NC)
        y_sq = th_sq[:, :].rearrange("p (h v) -> p h v", v=K)
        h2 = sb("h2", [P, NC, GT])
        h_res = sb("h_res", [P, 2, NC, GT])
        cent = sb("cent", [P, NC, GT])
        sq_xxx = sb("sq_xxx", [P, NC, GT])
        v_rest = sq_xxx
        rstd = sb("rstd", [P, GT])
        xn = sb("xn", [P, NC, GB, T + 1])
        sx = sb("sx", [P, NC, GT])
        m_a = sb("m_a", [P, GT])
        m_b = sb("m_b", [LORA, GT])
        mixed = sb("mixed", [P, 2, NC, GT])
        x_f = sb("x_f", [P, NMIX, NC, GT])
        td_h = sb("td_h", [DW, GT])
        w_s = sb("w_s", [P, 2, NC, GB, T])
        k_s = sb("k_s", [P, 2, NC, GT])
        r_s = sb("r_s", [P, 2, NC, GB, T])
        v_f = sb("v_f", [P, NC, GT])
        v_p = [sb(f"v_p{n}", [P, 2, NC, GT], BF16) for n in range(3)]
        rk = sb("rk", [P, NC, GT])
        gate = sb("gate", [P, 2, NC, GT])
        ruk = sb("ruk", [P, GB * H])
        y_now = sb("y_now", [P, 2, GB * H, K])
        kv = sb("kv", [P, RING, GT])
        state = sb("state", [P, RING, GT + 1])
        rs = sb("rs", [P, RING, GT])
        y = sb("y", [P, GB * H, K])
        mu = sb("mu", [P, GB * H])
        y_var = sb("y_var", [P, GB * H])
        z = sb("z", [P, NC, GT])
        rows = sb("rows", [P, GB, C])

        bank = [ps(f"front{n}", [P, 512]) for n in range(FRONT_BANKS)]
        tail_bank = ps("tail_bank", [P, 512])
        vrep = [ps(f"vrep{n}", [P, 512]) for n in range(2)]
        y_ps = ps("y_ps", [P, GB, C])

        w_ready = ready
        made = sem("made")
        front_filled = [sem(f"front_filled{n}") for n in range(FRONT_BANKS)]
        front_read = [sem(f"front_read{n}") for n in range(FRONT_BANKS)]
        tail_filled = sem("tail_filled")
        tail_read = sem("tail_read")
        x_loaded = [sem(f"x_loaded{n}") for n in range(2)]
        diff_ready = sem("diff_ready")
        summ_ready = sem("summ_ready")
        gated = sem("gated")
        h_ready = sem("h_ready")
        res_ready = sem("res_ready")
        squared = sem("squared")
        rstd_ready = sem("rstd_ready")
        xn_ready = sem("xn_ready")
        sx_ready = sem("sx_ready")
        xxx_ready = sem("xxx_ready")
        xf_ready = sem("xf_ready")
        decay_ready = sem("decay_ready")
        r_ready = sem("r_ready")
        tg_ready = sem("tg_ready")
        v_part = [sem(f"v_part{n}") for n in range(3)]
        rest_ready = sem("rest_ready")
        vrep_ready = sem("vrep_ready")
        kv_ready = sem("kv_ready")
        scanned = sem("scanned")
        rs_ready = sem("rs_ready")
        y_part = sem("y_part")
        y_read = sem("y_read")
        mu_ready = sem("mu_ready")
        y_cent = sem("y_cent")
        y_squared = sem("y_squared")
        yvar_sum = sem("yvar_sum")
        yvar_eps = sem("yvar_eps")
        yrstd_ready = sem("yrstd_ready")
        yn_ready = sem("yn_ready")
        z_ready = sem("z_ready")
        stored = sem("stored")

        x_dram = d["x"].rearrange("a (c p) n -> p (a c) n", p=P)
        out_dram = d["out"].rearrange("b t c -> t b c")

        def filled(eng, use, g):
            k = FRONT_INDEX[use]
            wait(eng, front_filled[k % FRONT_BANKS], g * FRONT_TURNS + (k // FRONT_BANKS + 1))

        def was_read(eng, use, g):
            k = FRONT_INDEX[use]
            wait(eng, front_read[k % FRONT_BANKS], g * FRONT_TURNS + (k // FRONT_BANKS + 1))

        def free(eng, use, g):
            k = FRONT_INDEX[use]
            wait(eng, front_read[k % FRONT_BANKS], g * FRONT_TURNS + k // FRONT_BANKS)

        def bank_of(use):
            return bank[FRONT_INDEX[use] % FRONT_BANKS]

        def fill_sem(use):
            return front_filled[FRONT_INDEX[use] % FRONT_BANKS]

        def read_sem(use):
            return front_read[FRONT_INDEX[use] % FRONT_BANKS]

        def by_seq(ap):
            return ap.rearrange("p (b t) -> p b t", b=GB)

        block = ctx.enter_context(nc.Block())

        @block.sync
        def _(sp):
            weights = [(w_tok, "tok_w"), (w_r, "Wr"), (w_k, "Wk"), (w_v, "Wv"), (w_g, "Wg"), (w_o, "Wo"),
                       (tm_w1, "tm_w1"), (td_w1, "td_w1")]

            def load(g, par):
                sp.dma_start(x_in[:, par], x_dram[:, :, bass.ds(g * GT, GT)]).then_inc(x_loaded[par], 16)

            load(0, 0)
            for tile, name in weights:
                sp.dma_start(tile[:], d[name].rearrange("(c p) n -> p c n", p=P)).then_inc(w_ready, 16)
            sp.dma_start(tm_w2[:], d["tm_w2"][0:P, :]).then_inc(w_ready, 16)
            sp.dma_start(tm_w2_last[:], d["tm_w2"][P:P + LORA, :]).then_inc(w_ready, 16)
            sp.dma_start(td_w2[:], d["td_w2"]).then_inc(w_ready, 16)
            sp.dma_start(head_sel[:], d["head_sel"]).then_inc(w_ready, 16)
            sp.dma_start(value_sel[:], d["value_sel"].rearrange("p (v q) -> p v q", v=K)).then_inc(w_ready, 16)

            def slot(u, scan, front, tail):
                if u == 0 and front is not None:
                    g, par, half = front
                    if not (isinstance(g, int) and g + 1 >= NG):
                        wait(sp, diff_ready, g)
                        wait(sp, summ_ready, g)
                        load(g + 1, 1 - par)
                if u == 16 and tail is not None:
                    g, par, half = tail
                    wait(sp, tail_read, g * 4 + 4)
                    sp.dma_start(out_dram[:, bass.ds(g * GB, GB), :], rows[0:T]).then_inc(stored, 16)

            walk(sp, slot)
            sp.wait_ge(stored, 16 * NG)

        @block.tensor
        def _(pe):
            pe.wait_ge(w_ready, 16 * 15)
            pe.wait_ge(made, 11)

            def dense(use, g, weights, moving, m=P, cols=None):
                free(pe, use, g)
                for c in range(NC):
                    last = nc.tensor.matmul(bank_of(use)[0:m, 0:GT], weights(c), moving(c),
                                            start=(c == 0), stop=(c == NC - 1))
                last.then_inc(fill_sem(use), 1)

            def project(name, weight, f, g):
                for o in range(NC):
                    dense(f"{name}{o}", g, lambda c: weight[:, c, o * P:(o + 1) * P], lambda c: x_f[:, f, c, :])

            def ysum(u, g):
                c, v = divmod(u, K)
                wait(pe, rs_ready, g * UNITS + u + 1)
                if u == 0:
                    wait(pe, y_read, g)
                for b in range(GB):
                    last = nc.tensor.matmul(y_ps[0:T, b, c * P + v:(c + 1) * P:K],
                                            rs[:, u % RING, b * T:(b + 1) * T], head_sel[:], start=True, stop=True)
                last.then_inc(y_part, 1)

            def slot(u, scan, front, tail):
                if scan is not None:
                    g, par, half = scan
                    c, v = divmod(u, K)
                    if u == 0:
                        wait(pe, v_part[2], g + 1)
                    wait(pe, kv_ready, g * UNITS + u - 1)
                    for n in range(3):
                        last = nc.tensor.matmul(vrep[u % 2][:, 0:GT], value_sel[:, v, :], v_p[n][:, par, c, :],
                                                start=(n == 0), stop=(n == 2))
                    last.then_inc(vrep_ready, 1)
                    if u >= 3:
                        ysum(u - 3, g)
                if u < 3 and tail is not None:
                    ysum(UNITS - 3 + u, tail[0])
                if front is not None:
                    g, par, half = front
                    if u == 1:
                        wait(pe, diff_ready, g + 1)
                        for o in range(NC):
                            dense(f"tok{o}", g, lambda c: w_tok[:, c, o * P:(o + 1) * P], lambda c: diff[:, c, :])
                    if u == 3:
                        wait(pe, h_ready, g + 1)
                        dense("mean", g, lambda c: mean_w[:], lambda c: h2[:, c, :])
                    if u == 5:
                        wait(pe, squared, g + 1)
                        dense("var", g, lambda c: mean_w[:], lambda c: sq_xxx[:, c, :])
                    if u == 9:
                        wait(pe, xxx_ready, g * NC + NC)
                        dense("m", g, lambda c: tm_w1[:, c, 0:P], lambda c: sq_xxx[:, c, :])
                        dense("m4", g, lambda c: tm_w1[:, c, P:P + LORA], lambda c: sq_xxx[:, c, :], m=LORA)
                    if 10 <= u < 10 + NMIX:
                        f = u - 10
                        if f == 0:
                            was_read(pe, "m", g)
                        if f == NMIX - 1:
                            was_read(pe, "m4", g)
                        for c in range(NC):
                            use = f"delta{f}{c}"
                            free(pe, use, g)
                            cols = slice(c * P, (c + 1) * P)
                            if f < NMIX - 1:
                                part = slice(f * LORA, (f + 1) * LORA)
                                w2, m = tm_w2[part, cols], m_a[part, :]
                            else:
                                w2, m = tm_w2_last[:, cols], m_b[:]
                            nc.tensor.matmul(bank_of(use)[:, 0:GT], w2, m, start=True, stop=True) \
                                .then_inc(fill_sem(use), 1)
                    if u == 16:
                        wait(pe, xf_ready, g * NMIX + 1)
                        dense("td", g, lambda c: td_w1[:, c, :], lambda c: x_f[:, 0, c, :], m=DW)
                    if u == 17:
                        was_read(pe, "td", g)
                        for c in range(NC):
                            use = f"ww{c}"
                            free(pe, use, g)
                            nc.tensor.matmul(bank_of(use)[:, 0:GT], td_w2[:, c * P:(c + 1) * P], td_h[:],
                                             start=True, stop=True).then_inc(fill_sem(use), 1)
                    if u == 18:
                        wait(pe, xf_ready, g * NMIX + 2)
                        project("k", w_k, 1, g)
                    if u == 19:
                        wait(pe, xf_ready, g * NMIX + 3)
                        project("v", w_v, 2, g)
                    if u == 20:
                        wait(pe, xf_ready, g * NMIX + 4)
                        project("r", w_r, 3, g)
                    if u == 21:
                        wait(pe, xf_ready, g * NMIX + 5)
                        project("g", w_g, 4, g)
                    if u == 23:
                        free(pe, "ruk", g)
                        was_read(pe, "r0", g)
                        was_read(pe, "r1", g)
                        for b in range(GB):
                            for c in range(NC):
                                at = b * H + c * HC
                                last = nc.tensor.matmul(bank_of("ruk")[0:T, at:at + HC],
                                                        rk[:, c, b * T:(b + 1) * T], head_u[:, c, :],
                                                        start=True, stop=True)
                        last.then_inc(fill_sem("ruk"), 1)
                    if u == 24:
                        for j in range(2):
                            use = f"vrow{j}"
                            free(pe, use, g)
                            if j == 0:
                                was_read(pe, "v0", g)
                                was_read(pe, "v1", g)
                            for b in range(2):
                                for c in range(NC):
                                    at = b * C + c * P
                                    seq = slice((2 * j + b) * T, (2 * j + b + 1) * T)
                                    last = nc.tensor.transpose(bank_of(use)[0:T, at:at + P], v_f[:, c, seq],
                                                               ident[:])
                            last.then_inc(fill_sem(use), 1)
                if tail is not None:
                    g, par, half = tail
                    if u in (10, 11):
                        c = u - 10
                        if c == 0:
                            wait(pe, yn_ready, g + 1)
                        wait(pe, tail_read, g * 4 + c)
                        for b in range(GB):
                            last = nc.tensor.transpose(
                                tail_bank[:, b * T:(b + 1) * T],
                                y[0:T, b * H + c * HC:b * H + (c + 1) * HC, :].rearrange("p h v -> p (h v)"),
                                ident[0:T, 0:T])
                        last.then_inc(tail_filled, 1)
                    if u in (13, 14):
                        j = u - 13
                        if j == 0:
                            wait(pe, z_ready, g + 1)
                            wait(pe, res_ready, g + 1)
                        wait(pe, tail_read, g * 4 + 2 + j)
                        for b in range(2):
                            seq = slice((2 * j + b) * T, (2 * j + b + 1) * T)
                            for c in range(NC):
                                nc.tensor.matmul(tail_bank[0:T, b * C:(b + 1) * C], z[:, c, seq], w_o[:, c, :],
                                                 start=(c == 0), stop=False, skip_group_check=True)
                            for c in range(NC):
                                at = b * C + c * P
                                last = nc.tensor.matmul(tail_bank[0:T, at:at + P], h_res[:, par, c, seq], ident[:],
                                                        start=False, stop=(c == NC - 1), skip_group_check=True)
                        last.then_inc(tail_filled, 1)

            walk(pe, slot)

        @block.vector
        def _(dve):
            nc.vector.memset(mean_w[:], 1.0 / C).then_inc(made, 1)
            nc.vector.memset(eps4[:], 4 * EPS).then_inc(made, 1)
            nc.vector.memset(eps1[:], EPS).then_inc(made, 1)
            nc.vector.memset(w_s[:], 0.0).then_inc(made, 1)
            nc.vector.memset(r_s[:], 0.0).then_inc(made, 1)
            nc.vector.memset(state[:], 0.0).then_inc(made, 1)
            nc.vector.memset(xn[:], 0.0).then_inc(made, 1)
            dve.wait_ge(w_ready, 16 * 15)
            for c in range(NC):
                u_col = params[:, COL["u"] + c:COL["u"] + c + 1]
                nc.vector.tensor_scalar(head_u[:, c, :], head_sel[:], u_col, None, ALU.mult).then_inc(made, 1)
            nc.vector.tensor_scalar(half_ln[:], params[:, COL["ln_w"]:COL["ln_w"] + 2 * NC], 0.5, None,
                                    ALU.mult).then_inc(made, 1)
            dve.wait_ge(made, 11)

            def scan_unit(u, g, par):
                c = u // K
                if u == 0:
                    wait(dve, decay_ready, g * NC + NC)
                wait(dve, kv_ready, g * UNITS + u + 1)
                wait(dve, rs_ready, g * UNITS + u + 1 - RING)
                nc.vector.tensor_tensor_scan(state[:, u % RING, 1:GT + 1],
                                             w_s[:, par, c].rearrange("p b t -> p (b t)"), kv[:, u % RING, :],
                                             0.0, ALU.mult, ALU.add).then_inc(scanned, 1)

            def slot(u, scan, front, tail):
                if scan is not None:
                    g, par, half = scan
                    c = u // K
                    if u == 0:
                        was_read(dve, "k0", g)
                        was_read(dve, "k1", g)
                    wait(dve, vrep_ready, g * UNITS + u + 1)
                    wait(dve, scanned, g * UNITS + u + 1 - RING)
                    nc.vector.tensor_tensor(kv[:, u % RING, :], vrep[u % 2][:, 0:GT], k_s[:, par, c, :],
                                            ALU.mult).then_inc(kv_ready, 1)
                    if u >= 1:
                        scan_unit(u - 1, g, par)
                if u == 0 and tail is not None:
                    scan_unit(UNITS - 1, tail[0], tail[1])
                if front is not None:
                    g, par, half = front
                    if u == 2:
                        was_read(dve, "tok0", g)
                        was_read(dve, "tok1", g)
                        nc.vector.tensor_tensor(th[:], th[:], diff[:], ALU.mult).then_inc(gated, 1)
                    if u == 3:
                        wait(dve, gated, g + 1)
                        wait(dve, summ_ready, g + 1)
                        wait(dve, res_ready, g)
                        nc.vector.tensor_tensor(h2[:], th[:], summ[:], ALU.add).then_inc(h_ready, 1)
                    if u == 4:
                        filled(dve, "mean", g)
                        mean = bank_of("mean")[:, 0:GT].unsqueeze(1).to_broadcast([P, NC, GT])
                        nc.vector.tensor_tensor(cent[:], h2[:], mean, ALU.subtract).then_inc(read_sem("mean"), 1)
                    if u == 6:
                        wait(dve, rstd_ready, g + 1)
                        wait(dve, xf_ready, g * NMIX)
                        for c in range(NC):
                            last = nc.vector.tensor_tensor(xn[:, c, :, 1:T + 1], by_seq(cent[:, c, :]),
                                                           by_seq(rstd[:]), ALU.mult)
                        last.then_inc(xn_ready, 1)
                    if u == 8:
                        wait(dve, sx_ready, g + 1)
                        for c in range(NC):
                            maa_x = params[:, COL["maa_x"] + c:COL["maa_x"] + c + 1]
                            nc.vector.scalar_tensor_tensor(by_seq(sq_xxx[:, c, :]), by_seq(sx[:, c, :]), maa_x,
                                                           xn[:, c, :, 1:T + 1], ALU.mult, ALU.add) \
                                .then_inc(xxx_ready, 1)
                    if 11 <= u < 11 + NMIX:
                        f = u - 11
                        wait(dve, xf_ready, g * NMIX + f - 1)
                        for c in range(NC):
                            use = f"delta{f}{c}"
                            maa = params[:, COL["maa"] + f * NC + c:COL["maa"] + f * NC + c + 1]
                            filled(dve, use, g)
                            nc.vector.scalar_tensor_tensor(mixed[:, f % 2, c, :], bank_of(use)[:, 0:GT], maa,
                                                           sx[:, c, :], ALU.add, ALU.mult) \
                                .then_inc(read_sem(use), 1)
                    if u == 21:
                        was_read(dve, "k0", g)
                        was_read(dve, "k1", g)
                        for c in range(NC):
                            use = f"r{c}"
                            wait(dve, r_ready, g * NC + c + 1)
                            nc.vector.tensor_tensor(rk[:, c, :], bank_of(use)[:, 0:GT], k_s[:, par, c, :],
                                                    ALU.mult).then_inc(read_sem(use), 1)
                    if u == 22:
                        for c in range(NC):
                            use = f"g{c}"
                            wait(dve, tg_ready, g * NC + c + 1)
                            nc.vector.scalar_tensor_tensor(gate[:, par, c, :], gate[:, par, c, :], 1.0,
                                                           bank_of(use)[:, 0:GT], ALU.add, ALU.mult) \
                                .then_inc(read_sem(use), 1)
                    if u in (25, 26):
                        j = u - 25
                        use = f"vrow{j}"
                        if j == 0:
                            was_read(dve, "ruk", g)
                        filled(dve, use, g)
                        heads = slice(j * 2 * H, (j + 1) * 2 * H)
                        nc.vector.tensor_tensor(y_now[0:T, par, heads, :],
                                                bank_of(use)[0:T, :].rearrange("p (h v) -> p h v", v=K),
                                                ruk[0:T, heads].unsqueeze(2).to_broadcast([T, 2 * H, K]),
                                                ALU.mult).then_inc(read_sem(use), 1)
                if tail is not None:
                    g, par, half = tail
                    heads_of = [T, GB * H, K]
                    if u == 3:
                        wait(dve, y_part, g * UNITS + UNITS)
                        was_read(dve, "vrow1", g)
                        if front is None:
                            wait(dve, tail_filled, g * 4 - 2)
                        nc.vector.tensor_tensor(y[0:T], y_ps[0:T].rearrange("p b (h v) -> p (b h) v", v=K),
                                                y_now[0:T, par], ALU.add).then_inc(y_read, 1)
                    if u == 4:
                        wait(dve, y_read, g + 1)
                        nc.vector.tensor_reduce(mu[0:T], y[0:T], AX_X, ALU.add).then_inc(mu_ready, 1)
                    if u == 5:
                        wait(dve, mu_ready, g + 1)
                        nc.vector.scalar_tensor_tensor(y[0:T], mu[0:T].unsqueeze(2).to_broadcast(heads_of),
                                                       -1.0 / K, y[0:T], ALU.mult, ALU.add).then_inc(y_cent, 1)
                    if u == 7:
                        wait(dve, y_squared, g + 1)
                        nc.vector.tensor_reduce(y_var[0:T], y_sq[0:T], AX_X, ALU.add).then_inc(yvar_sum, 1)
                    if u == 9:
                        wait(dve, yrstd_ready, g + 1)
                        nc.vector.tensor_tensor(y[0:T], y[0:T], y_var[0:T].unsqueeze(2).to_broadcast(heads_of),
                                                ALU.mult).then_inc(yn_ready, 1)

            walk(dve, slot)

        @block.gpsimd
        def _(pool):
            nc.gpsimd.memset(neg_half[:], -0.5).then_inc(made, 1)
            pool.wait_ge(made, 11)

            def rs_unit(u, g, par):
                wait(pool, scanned, g * UNITS + u + 1)
                if u == 0:
                    wait(pool, r_ready, g * NC + NC)
                wait(pool, y_part, g * UNITS + u + 1 - RING)
                nc.gpsimd.tensor_tensor(rs[:, u % RING, :], r_s[:, par, u // K].rearrange("p b t -> p (b t)"),
                                        state[:, u % RING, 0:GT], ALU.mult).then_inc(rs_ready, 1)

            def slot(u, scan, front, tail):
                if scan is not None and u >= 2:
                    rs_unit(u - 2, scan[0], scan[1])
                if u < 2 and tail is not None:
                    rs_unit(UNITS - 2 + u, tail[0], tail[1])
                if front is not None:
                    g, par, half = front
                    if u == 0:
                        wait(pool, x_loaded[par], half * 16 + 16)
                        wait(pool, h_ready, g)
                        nc.gpsimd.tensor_tensor(diff[:], x_in[:, par, 0:NC], x_in[:, par, NC:2 * NC],
                                                ALU.subtract).then_inc(diff_ready, 1)
                        nc.gpsimd.tensor_tensor(summ[:], x_in[:, par, 0:NC], x_in[:, par, NC:2 * NC],
                                                ALU.add).then_inc(summ_ready, 1)
                    if u == 5:
                        was_read(pool, "var", g)
                        nc.gpsimd.tensor_tensor(rstd[:], rstd[:], neg_half[:].to_broadcast([P, GT]),
                                                ALU.pow).then_inc(rstd_ready, 1)
                    if u == 7:
                        wait(pool, xn_ready, g + 1)
                        for c in range(NC):
                            last = nc.gpsimd.tensor_tensor(by_seq(sx[:, c, :]), xn[:, c, :, 0:T],
                                                           xn[:, c, :, 1:T + 1], ALU.subtract)
                        last.then_inc(sx_ready, 1)
                    if 12 <= u < 12 + NMIX:
                        f = u - 12
                        was_read(pool, f"delta{f}0", g)
                        was_read(pool, f"delta{f}1", g)
                        if f == 0:
                            filled(pool, "g1", g - 1)
                        for c in range(NC):
                            last = nc.gpsimd.tensor_tensor(by_seq(x_f[:, f, c, :]), by_seq(mixed[:, f % 2, c, :]),
                                                           xn[:, c, :, 1:T + 1], ALU.add)
                        last.then_inc(xf_ready, 1)
                    if u == 21:
                        wait(pool, v_part[0], g + 1)
                        nc.gpsimd.tensor_tensor(v_rest[:], v_f[:], v_p[0][:, par], ALU.subtract) \
                            .then_inc(rest_ready, 1)
                    if u == 23:
                        wait(pool, v_part[1], g + 1)
                        wait(pool, rest_ready, g + 1)
                        wait(pool, vrep_ready, g * UNITS - UNITS)
                        nc.gpsimd.tensor_tensor(v_p[2][:, par], v_rest[:], v_p[1][:, par], ALU.subtract) \
                            .then_inc(v_part[2], 1)
                if tail is not None:
                    g, par, half = tail
                    if u == 8:
                        wait(pool, yvar_eps, g + 1)
                        nc.gpsimd.tensor_tensor(y_var[0:T], y_var[0:T], neg_half[0:T].to_broadcast([T, GB * H]),
                                                ALU.pow).then_inc(yrstd_ready, 1)
                    if u == 12:
                        wait(pool, tail_read, g * 4 + 2)
                        nc.gpsimd.tensor_tensor(z[:], z[:], gate[:, par], ALU.mult).then_inc(z_ready, 1)

            walk(pool, slot)

        @block.scalar
        def _(act):
            act.wait_ge(w_ready, 16 * 15)
            act.wait_ge(made, 11)

            def column(name, c):
                return params[:, COL[name] + c:COL[name] + c + 1]

            def slot(u, scan, front, tail):
                if front is not None:
                    g, par, half = front
                    if u == 1:
                        wait(act, h_ready, g)
                        for c in range(NC):
                            use = f"tok{c}"
                            filled(act, use, g)
                            nc.scalar.activation(th[:, c, :], bank_of(use)[:, 0:GT], ACT.Tanh, scale=0.5) \
                                .then_inc(read_sem(use), 1)
                    if u == 4:
                        was_read(act, "mean", g)
                        nc.scalar.activation(sq_xxx[:], cent[:], ACT.Square).then_inc(squared, 1)
                    if u == 5:
                        filled(act, "var", g)
                        wait(act, xn_ready, g)
                        nc.scalar.activation(rstd[:], bank_of("var")[:, 0:GT], ACT.Identity, bias=eps4[:]) \
                            .then_inc(read_sem("var"), 1)
                    if u == 9:
                        filled(act, "m", g)
                        nc.scalar.activation(m_a[:], bank_of("m")[:, 0:GT], ACT.Tanh).then_inc(read_sem("m"), 1)
                        filled(act, "m4", g)
                        nc.scalar.activation(m_b[:], bank_of("m4")[0:LORA, 0:GT], ACT.Tanh) \
                            .then_inc(read_sem("m4"), 1)
                    if u == 16:
                        filled(act, "td", g)
                        nc.scalar.activation(td_h[:], bank_of("td")[0:DW, 0:GT], ACT.Tanh) \
                            .then_inc(read_sem("td"), 1)
                    if u == 17:
                        wait(act, scanned, g * UNITS - UNITS)
                        for c in range(NC):
                            use = f"ww{c}"
                            filled(act, use, g)
                            nc.scalar.activation(w_s[:, par, c, :, 1:T], by_seq(bank_of(use)[:, 0:GT])[:, :, 1:T],
                                                 ACT.Exp, bias=column("decay", c)).then_inc(read_sem(use), 1)
                        for c in range(NC):
                            was_read(act, f"ww{c}", g)
                            nc.scalar.activation(w_s[:, par, c, :, 1:T], w_s[:, par, c, :, 1:T], ACT.Exp,
                                                 scale=-1.0).then_inc(decay_ready, 1)
                    if u == 18:
                        wait(act, kv_ready, g * UNITS - UNITS)
                        for c in range(NC):
                            use = f"k{c}"
                            filled(act, use, g)
                            nc.scalar.copy(k_s[:, par, c, :], bank_of(use)[:, 0:GT]).then_inc(read_sem(use), 1)
                    if u == 19:
                        wait(act, v_part[2], g)
                        filled(act, "vrow1", g - 1)
                        for c in range(NC):
                            use = f"v{c}"
                            filled(act, use, g)
                            nc.scalar.copy(v_f[:, c, :], bank_of(use)[:, 0:GT]).then_inc(read_sem(use), 1)
                        was_read(act, "v0", g)
                        was_read(act, "v1", g)
                        wait(act, vrep_ready, g * UNITS - UNITS)
                        nc.scalar.copy(v_p[0][:, par], v_f[:]).then_inc(v_part[0], 1)
                    if u == 20:
                        wait(act, rs_ready, g * UNITS - UNITS)
                        for c in range(NC):
                            use = f"r{c}"
                            filled(act, use, g)
                            nc.scalar.copy(r_s[:, par, c, :, 1:T], by_seq(bank_of(use)[:, 0:GT])[:, :, 1:T]) \
                                .then_inc(r_ready, 1)
                    if u == 21:
                        wait(act, z_ready, g - 1)
                        for c in range(NC):
                            use = f"g{c}"
                            filled(act, use, g)
                            nc.scalar.activation(gate[:, par, c, :], bank_of(use)[:, 0:GT], ACT.Tanh, scale=0.5) \
                                .then_inc(tg_ready, 1)
                    if u == 22:
                        wait(act, rest_ready, g + 1)
                        nc.scalar.copy(v_p[1][:, par], v_rest[:]).then_inc(v_part[1], 1)
                    if u == 23:
                        filled(act, "ruk", g)
                        nc.scalar.copy(ruk[0:T], bank_of("ruk")[0:T, 0:GB * H]).then_inc(read_sem("ruk"), 1)
                    if u == 24:
                        wait(act, tail_filled, g * 4 - 4)
                        nc.scalar.mul(h_res[:, par], h2[:], 0.5).then_inc(res_ready, 1)
                if tail is not None:
                    g, par, half = tail
                    if u == 6:
                        wait(act, y_cent, g + 1)
                        nc.scalar.activation(y_sq[0:T], y[0:T], ACT.Square).then_inc(y_squared, 1)
                    if u == 8:
                        wait(act, yvar_sum, g + 1)
                        nc.scalar.activation(y_var[0:T], y_var[0:T], ACT.Identity, bias=eps1[0:T], scale=1.0 / K) \
                            .then_inc(yvar_eps, 1)
                    if u in (10, 11):
                        c = u - 10
                        wait(act, tail_filled, g * 4 + c + 1)
                        nc.scalar.activation(z[:, c, :], tail_bank[:, 0:GT], ACT.Identity,
                                             bias=half_ln[:, NC + c:NC + c + 1], scale=half_ln[:, c:c + 1]) \
                            .then_inc(tail_read, 1)
                    if u in (14, 15):
                        j = u - 14
                        wait(act, tail_filled, g * 4 + j + 3)
                        if j == 0:
                            wait(act, stored, g * 16)
                        nc.scalar.copy(rows[0:T, 2 * j:2 * j + 2, :],
                                       tail_bank[0:T, :].rearrange("p (b c) -> p b c", b=2)) \
                            .then_inc(tail_read, 1)

            walk(act, slot)


def expert_phase(nc, d, const):
    ident, params, ready = const
    with ExitStack() as ctx:
        def sb(name, shape, dt=F32):
            return ctx.enter_context(nc.sbuf_tensor(name, shape, dt))

        def ps(name, shape):
            return ctx.enter_context(nc.psum_tensor(name, shape, F32))

        def sem(name):
            return ctx.enter_context(nc.semaphore(name))

        idx = sb("idx", [P, NT], I32)
        idx_f = sb("idx_f", [P, NT])
        spare = sb("spare", [P, 1])
        earlier = sb("earlier", [P, P])
        ones_row = sb("ones_row", [1, P])
        b1 = sb("b1", [P, E, NF])
        b2 = sb("b2", [1, E, C])
        w1 = sb("w1", [P, 2, NC, FF])
        w2 = sb("w2", [P, 2, NF, C])
        got = sb("got", [P, NT, C])
        got_w = sb("got_w", [P, NT, E])
        stats = sb("stats", [P, NT, 6])
        moments = sb("moments", [P, NT, 2])
        rstd = sb("rstd2", [P, NT])
        neg_half = sb("neg_half2", [P, 1])
        normed = sb("normed", [P, 2, C])
        xT = sb("xT", [P, 2, NC, CAP])
        hid = sb("hid", [P, NF, CAP])
        weighted = sb("weighted", [P, 2, C])
        same = sb("same", [P, 2, P])
        same_before = sb("same_before", [P, P])
        dups = sb("dups", [P, NT])
        target_f = sb("target_f", [P, NT])
        shift_f = sb("shift_f", [P, NT])
        target = sb("target", [P, NT], I32)
        summed = sb("summed", [P, 2, C])
        zero = sb("zero", [P, C])

        t_ps = [ps(f"t_ps{n}", [P, 512]) for n in range(2)]
        h_ps = [ps(f"h_ps{n}", [P, 512]) for n in range(2)]
        o_ps = [ps(f"o_ps{n}", [P, 512]) for n in range(2)]
        i_ps = ps("i_ps", [P, 512])
        s_ps = ps("s_ps", [P, 512])

        loaded = sem("e_loaded")
        w_loaded = [sem(f"e_w_loaded{n}") for n in range(2)]
        table_ready = sem("table_ready")
        gathered = sem("gathered")
        made = sem("e_made")
        zero_ready = sem("zero_ready")
        power_ready = sem("power_ready")
        stats_ready = sem("stats_ready")
        moments_ready = sem("moments_ready")
        var_ready = sem("e_var_ready")
        rstd_ready = sem("e_rstd_ready")
        normed_ready = sem("normed_ready")
        turned = sem("turned")
        xT_ready = sem("xT_ready")
        h_filled = sem("h_filled")
        h_read = sem("h_read")
        o_filled = sem("o_filled")
        weighted_ready = sem("weighted_ready")
        i_filled = sem("i_filled")
        same_ready = sem("same_ready")
        before_ready = sem("before_ready")
        dups_ready = sem("dups_ready")
        target_step = sem("target_step")
        s_filled = sem("s_filled")
        summed_ready = sem("summed_ready")
        scattered = sem("scattered")
        copied = sem("copied")

        out_rows = d["out"].rearrange("b t c -> (b t) c")
        table = d["table"]
        weight_rows = d["combine_weights"]
        w1_dram = d["W1"].rearrange("e (c p) f -> e p c f", p=P)
        w2_dram = d["W2"].rearrange("e (n p) c -> e p n c", p=P)

        block = ctx.enter_context(nc.Block())

        @block.sync
        def _(sp):
            sp.dma_start(idx[:], d["idx"]).then_inc(loaded, 16)
            sp.dma_start(spare[:], d["spare"]).then_inc(loaded, 16)
            sp.dma_start(earlier[:], d["earlier"]).then_inc(loaded, 16)
            sp.dma_start(b1[:], d["b1"].rearrange("p (e n) -> p e n", e=E)).then_inc(loaded, 16)
            sp.dma_start(b2[:], d["b2"].rearrange("(a e) c -> a e c", a=1)).then_inc(loaded, 16)
            sp.dma_start(table[0:NTOK, :], out_rows[0:NTOK, :]).then_inc(table_ready, 16)
            sp.wait_ge(zero_ready, 1)
            sp.dma_start(table[NTOK:TABLE, :], zero[:]).then_inc(table_ready, 16)
            for e in range(E):
                if e >= 2:
                    sp.wait_ge(o_filled, TPE * (e - 1))
                sp.dma_start(w1[:, e % 2], w1_dram[e]).then_inc(w_loaded[e % 2], 16)
                sp.dma_start(w2[:, e % 2], w2_dram[e]).then_inc(w_loaded[e % 2], 16)
            sp.wait_ge(scattered, 16 * NT)
            sp.dma_start(out_rows[0:NTOK, :], table[0:NTOK, :]).then_inc(copied, 16)
            sp.wait_ge(copied, 16)

        @block.gpsimd
        def _(pool):
            nc.gpsimd.memset(zero[:], 0.0).then_inc(zero_ready, 1)
            nc.gpsimd.memset(neg_half[:], -0.5).then_inc(power_ready, 1)
            pool.wait_ge(loaded, 16 * 5)
            for t in range(NT):
                at = bass.IndirectOffsetOnAxis(ap=idx[:, t:t + 1], axis=0)
                nc.gpsimd.indirect_dma_start(out=got[:, t, :], out_offset=None, in_=out_rows[:],
                                             in_offset=at).then_inc(gathered, 16)
                nc.gpsimd.indirect_dma_start(out=got_w[:, t, :], out_offset=None, in_=weight_rows[:],
                                             in_offset=at).then_inc(gathered, 16)
            pool.wait_ge(var_ready, 1)
            pool.wait_ge(power_ready, 1)
            nc.gpsimd.tensor_tensor(rstd[:], rstd[:], neg_half[:].to_broadcast([P, NT]), ALU.pow) \
                .then_inc(rstd_ready, 1)
            pool.wait_ge(table_ready, 32)
            pool.wait_ge(target_step, 4)
            for t in range(NT):
                pool.wait_ge(summed_ready, t + 1)
                if t >= 1:
                    pool.wait_ge(scattered, 16 * t)
                nc.gpsimd.indirect_dma_start(
                    out=table[:], out_offset=bass.IndirectOffsetOnAxis(ap=target[:, t:t + 1], axis=0),
                    in_=summed[:, t % 2, :], in_offset=None, compute_op=ALU.add).then_inc(scattered, 16)

        @block.vector
        def _(dve):
            nc.vector.memset(ones_row[:], 1.0).then_inc(made, 1)
            dve.wait_ge(loaded, 16 * 5)
            nc.vector.tensor_copy(idx_f[:], idx[:]).then_inc(made, 1)
            dve.wait_ge(made, 2)
            for t in range(NT):
                dve.wait_ge(i_filled, t + 1)
                if t >= 1:
                    dve.wait_ge(dups_ready, t)
                nc.vector.scalar_tensor_tensor(same_before[:], i_ps[:, 0:P],
                                               idx_f[:, t:t + 1], earlier[:], ALU.is_equal, ALU.mult) \
                    .then_inc(before_ready, 1)
                dve.wait_ge(before_ready, t + 1)
                nc.vector.tensor_reduce(dups[:, t:t + 1], same_before[:], AX_X, ALU.max).then_inc(dups_ready, 1)
            dve.wait_ge(dups_ready, NT)
            nc.vector.tensor_scalar(shift_f[:], idx_f[:], spare[:, 0:1], -1.0, ALU.subtract, ALU.mult) \
                .then_inc(target_step, 1)
            dve.wait_ge(target_step, 1)
            nc.vector.tensor_tensor(shift_f[:], shift_f[:], dups[:], ALU.mult).then_inc(target_step, 1)
            dve.wait_ge(target_step, 2)
            nc.vector.tensor_tensor(target_f[:], shift_f[:], idx_f[:], ALU.add).then_inc(target_step, 1)
            dve.wait_ge(target_step, 3)
            nc.vector.tensor_copy(target[:], target_f[:]).then_inc(target_step, 1)
            dve.wait_ge(gathered, 32 * NT)
            for t in range(NT):
                nc.vector.bn_stats(stats[:, t, :], got[:, t, :]).then_inc(stats_ready, 1)
            for t in range(NT):
                dve.wait_ge(stats_ready, t + 1)
                nc.vector.bn_aggr(moments[:, t, :], stats[:, t, :]).then_inc(moments_ready, 1)
            dve.wait_ge(moments_ready, NT)
            nc.vector.tensor_scalar(rstd[:], moments[:, :, 1], EPS, None, ALU.add).then_inc(var_ready, 1)
            dve.wait_ge(rstd_ready, 1)

            def normalise(t):
                if t >= 2:
                    dve.wait_ge(turned, t - 1)
                nc.vector.tensor_scalar(normed[:, t % 2, :], got[:, t, :], moments[:, t, 0:1], rstd[:, t:t + 1],
                                        ALU.subtract, ALU.mult).then_inc(normed_ready, 1)

            def collect(t):
                if t >= 2:
                    dve.wait_ge(s_filled, t - 1)
                nc.vector.tensor_scalar(same[:, t % 2, :], i_ps[:, 0:P],
                                        idx_f[:, t:t + 1], None, ALU.is_equal).then_inc(same_ready, 1)

            def take(t):
                dve.wait_ge(s_filled, t + 1)
                if t >= 2:
                    dve.wait_ge(scattered, 16 * (t - 1))
                nc.vector.tensor_copy(summed[:, t % 2, :], s_ps[:, 0:C]).then_inc(summed_ready, 1)

            for e in range(E):
                if e == 0:
                    for t in range(TPE):
                        normalise(t)
                if e + 1 < E:
                    for j in range(TPE):
                        normalise((e + 1) * TPE + j)
                for j in range(TPE):
                    t = e * TPE + j
                    dve.wait_ge(i_filled, NT + t + 1)
                    collect(t)
                    take(t)

        @block.tensor
        def _(pe):
            pe.wait_ge(made, 2)

            def turn_index(t):
                nc.tensor.transpose(i_ps[:, 0:P], idx_f[:, t:t + 1].to_broadcast([P, P]),
                                    ident[:]).then_inc(i_filled, 1)

            def turn_rows(e):
                for j in range(TPE):
                    t = e * TPE + j
                    pe.wait_ge(normed_ready, t + 1)
                    if j == 0 and e >= 1:
                        pe.wait_ge(xT_ready, NC * e)
                    for c in range(NC):
                        last = nc.tensor.transpose(t_ps[c][:, j * P:(j + 1) * P], normed[:, t % 2, c * P:(c + 1) * P],
                                                   ident[:])
                    last.then_inc(turned, 1)

            for t in range(NT):
                if t >= 1:
                    pe.wait_ge(before_ready, t)
                turn_index(t)
            turn_rows(0)
            for e in range(E):
                pe.wait_ge(xT_ready, NC * (e + 1))
                pe.wait_ge(w_loaded[e % 2], 32 * (e // 2 + 1))
                for n in range(NF):
                    q = e * NF + n
                    if q >= 2:
                        pe.wait_ge(h_read, q - 1)
                    for c in range(NC):
                        last = nc.tensor.matmul(h_ps[q % 2][:], w1[:, e % 2, c, n * P:(n + 1) * P],
                                                xT[:, e % 2, c, :], start=(c == 0), stop=(c == NC - 1))
                    last.then_inc(h_filled, 1)
                if e >= 1:
                    sum_same(nc, pe, e * TPE - 1, same, weighted, s_ps, same_ready, weighted_ready, summed_ready, s_filled)
                if e + 1 < E:
                    turn_rows(e + 1)
                pe.wait_ge(h_read, NF * (e + 1))
                for j in range(TPE):
                    t = e * TPE + j
                    if t >= 2:
                        pe.wait_ge(weighted_ready, t - 1)
                    nc.tensor.matmul(o_ps[t % 2][:, 0:C], ones_row[:], b2[:, e, :], start=True, stop=False)
                    for n in range(NF):
                        last = nc.tensor.matmul(o_ps[t % 2][:, 0:C], hid[:, n, j * P:(j + 1) * P], w2[:, e % 2, n, :],
                                                start=False, stop=(n == NF - 1))
                    last.then_inc(o_filled, 1)
                    if t >= 1:
                        pe.wait_ge(same_ready, t)
                    else:
                        pe.wait_ge(dups_ready, NT)
                    turn_index(t)
                    if j >= 1:
                        sum_same(nc, pe, t - 1, same, weighted, s_ps, same_ready, weighted_ready, summed_ready, s_filled)
            sum_same(nc, pe, NT - 1, same, weighted, s_ps, same_ready, weighted_ready, summed_ready, s_filled)

        @block.scalar
        def _(act):
            def take_turned(e):
                act.wait_ge(turned, TPE * (e + 1))
                if e >= 2:
                    act.wait_ge(h_filled, NF * (e - 1))
                for c in range(NC):
                    nc.scalar.copy(xT[:, e % 2, c, :], t_ps[c][:]).then_inc(xT_ready, 1)

            act.wait_ge(loaded, 16 * 5)
            act.wait_ge(gathered, 32 * NT)
            take_turned(0)
            for e in range(E):
                if e >= 1:
                    act.wait_ge(o_filled, TPE * e)
                for n in range(NF):
                    q = e * NF + n
                    act.wait_ge(h_filled, q + 1)
                    nc.scalar.activation(hid[:, n, :], h_ps[q % 2][:], ACT.Gelu_apprx_tanh,
                                         bias=b1[:, e, n:n + 1]).then_inc(h_read, 1)
                if e + 1 < E:
                    take_turned(e + 1)
                for j in range(TPE):
                    t = e * TPE + j
                    act.wait_ge(o_filled, t + 1)
                    if t >= 2:
                        act.wait_ge(s_filled, t - 1)
                    nc.scalar.activation(weighted[:, t % 2, :], o_ps[t % 2][:, 0:C], ACT.Copy,
                                         scale=got_w[:, t, e:e + 1]).then_inc(weighted_ready, 1)


def sum_same(nc, pe, t, same, weighted, s_ps, same_ready, weighted_ready, summed_ready, s_filled):
    pe.wait_ge(same_ready, t + 1)
    pe.wait_ge(weighted_ready, t + 1)
    if t >= 1:
        pe.wait_ge(summed_ready, t)
    nc.tensor.matmul(s_ps[:, 0:C], same[:, t % 2, :], weighted[:, t % 2, :], start=True, stop=True) \
        .then_inc(s_filled, 1)


def build(nc, d):
    with ExitStack() as ctx:
        ident = ctx.enter_context(nc.sbuf_tensor("ident", [P, P], F32))
        params = ctx.enter_context(nc.sbuf_tensor("params", [P, NPAR], F32))
        ready = ctx.enter_context(nc.semaphore("w_ready"))
        with nc.Block() as block:
            @block.sync
            def _(sp):
                sp.dma_start(ident[:], d["ident"]).then_inc(ready, 16)
                sp.dma_start(params[:], d["params"]).then_inc(ready, 16)
        attention_phase(nc, d, (ident, params, ready))
        expert_phase(nc, d, (ident, params, ready))


def kernel(**inputs):
    import numpy as np
    import ml_dtypes
    import concourse.bacc as bacc
    from concourse.bass_utils import run_bass_kernel_spmd

    def get(name):
        return np.asarray(inputs[name])

    def columns(a):
        return a.reshape(-1, P).T

    attn = "L0_attn_"
    idx = get("L0_ffn_top_idx")
    if idx.dtype.itemsize == 8:
        idx = np.ascontiguousarray(idx).view(np.int32).reshape(CAP, E, 2)[:, :, 0]
    own = np.arange(P)
    arrays = {
        "x": get("x").reshape(B * T, 2, C).transpose(1, 2, 0),
        "tok_w": get("L0_tok_w"), "Wr": get(attn + "Wr"), "Wk": get(attn + "Wk"), "Wv": get(attn + "Wv"),
        "Wg": get(attn + "Wg"), "Wo": get(attn + "Wo"), "tm_w1": get(attn + "tm_w1"),
        "tm_w2": get(attn + "tm_w2").reshape(NMIX * LORA, C), "td_w1": get(attn + "td_w1"),
        "td_w2": get(attn + "td_w2"),
        "params": np.concatenate([columns(get(attn + n)) for n in
                                  ("time_maa_x", "time_maa_wkvrg", "time_decay", "time_faaaa", "ln_w", "ln_b")], 1),
        "ident": np.eye(P, dtype=np.float32),
        "head_sel": (own[:, None] // K == np.arange(HC)).astype(np.float32),
        "value_sel": ((own[:, None, None] // K == own // K)
                      & (own[:, None, None] % K == np.arange(K)[:, None])).astype(ml_dtypes.bfloat16).reshape(P, -1),
        "idx": idx.reshape(TPE, P, E).transpose(1, 2, 0).reshape(P, NT),
        "spare": (NTOK + own[:, None]).astype(np.float32),
        "earlier": (own < own[:, None]).astype(np.float32),
        "b1": get("L0_ffn_b1").reshape(E, NF, P).transpose(2, 0, 1).reshape(P, E * NF),
        "b2": get("L0_ffn_b2"), "W1": get("L0_ffn_W1"), "W2": get("L0_ffn_W2"),
        "combine_weights": get("L0_ffn_combine_weights"),
    }
    arrays = {"in_" + name: np.ascontiguousarray(a) for name, a in arrays.items()}
    nc = bacc.Bacc("TRN2", target_bir_lowering=False, num_devices=1)
    d = {name[3:]: nc.dram_tensor(name, a.shape, mybir.dt.from_np(a.dtype), kind="ExternalInput").ap()
         for name, a in arrays.items()}
    d["out"] = nc.dram_tensor("out", (B, T, C), F32, kind="ExternalOutput").ap()
    d["table"] = nc.dram_tensor("table", (TABLE, C), F32, kind="Internal").ap()
    build(nc, d)
    r = run_bass_kernel_spmd(nc, [arrays], core_ids=[0])
    return r.results[0]["out"]
```

```python
from contextlib import ExitStack

import concourse.bass as bass
from concourse import mybir

F32 = mybir.dt.float32
F32R = mybir.dt.float32r
I32 = mybir.dt.int32
ALU = mybir.AluOpType
ACT = mybir.ActivationFunctionType
AX_X = mybir.AxisListType.X

P = 128
C = 256
NC = C // P
T = 125
B = 128
GB = 4
GT = GB * T
NG = B // GB
H, K = 16, 16
HC = H // NC
LORA = 32
NMIX = 5
DW = 64
UNITS = NC * K
RING = 4
assert UNITS % RING == 0
EPS = 1e-5
E, CAP, FF, NTOK = 8, 512, 1024, 2048
NF = FF // P
TPE = CAP // P
NT = E * TPE
TABLE = NTOK + P

COL = {"maa_x": 0, "maa": NC, "decay": NC * 6, "u": NC * 7, "ln_w": NC * 8, "ln_b": NC * 9}
NPAR = NC * 10

FRONT_USES = (["tok0", "tok1", "mean", "var", "m", "m4"]
              + [f"delta{f}{c}" for f in range(NMIX) for c in range(NC)]
              + ["td", "v0", "v1", "ww0", "ww1", "k0", "k1", "r0", "r1", "g0", "g1"])
SLOT = {"tok0": 1, "tok1": 2, "mean": 5, "var": 7, "m": 12, "m4": 13, "delta": 14, "td": 19, "v0": 20, "v1": 21,
        "ww": 22, "k0": 23, "k1": 24, "r0": 25, "r1": 26, "g0": 27, "g1": 28, "ruk0": 29, "ruk1": 30}
FRONT_INDEX = {name: k for k, name in enumerate(FRONT_USES)}
FRONT_BANKS = 3
FRONT_TURNS = len(FRONT_USES) // FRONT_BANKS
assert len(FRONT_USES) % FRONT_BANKS == 0
TAIL_USES = ["cent0", "cent1", "var0", "var1", "rows0", "rows1"]
TU = len(TAIL_USES)


def wait(eng, sem, value):
    if isinstance(value, int) and value <= 0:
        return
    eng.wait_ge(sem, value)


def walk(eng, slot):
    def one(scan, front, tail):
        for u in range(UNITS):
            slot(u, scan, front, tail)

    def at(g):
        return (g, g % 2, g // 2) if 0 <= g < NG else None

    one(None, at(0), None)
    one(at(0), at(1), None)
    one(at(1), at(2), at(0))
    with eng.Fori(1, NG // 2 - 1) as i:
        one((i * 2, 0, i), (i * 2 + 1, 1, i), (i * 2 - 1, 1, i - 1))
        one((i * 2 + 1, 1, i), (i * 2 + 2, 0, i + 1), (i * 2, 0, i))
    for g in range(NG - 2, NG + 1):
        one(at(g), at(g + 1), at(g - 1))


def attention_phase(nc, d, const):
    ident, params, ready = const
    with ExitStack() as ctx:
        def sb(name, shape, dt=F32):
            return ctx.enter_context(nc.sbuf_tensor(name, shape, dt))

        def ps(name, shape):
            return ctx.enter_context(nc.psum_tensor(name, shape, F32))

        def sem(name):
            return ctx.enter_context(nc.semaphore(name))

        w_tok = sb("w_tok", [P, NC, C])
        w_r = sb("w_r", [P, NC, C])
        w_k = sb("w_k", [P, NC, C])
        w_v = sb("w_v", [P, NC, C])
        w_g = sb("w_g", [P, NC, C])
        w_o = sb("w_o", [P, NC, C])
        tm_w1 = sb("tm_w1", [P, NC, NMIX * LORA])
        tm_w2 = sb("tm_w2", [P, C])
        tm_w2_last = sb("tm_w2_last", [LORA, C])
        td_w1 = sb("td_w1", [P, NC, DW])
        td_w2 = sb("td_w2", [DW, C])
        head_u = sb("head_u", [P, NC, P])
        head_mean = sb("head_mean", [P, P])
        head_cent = sb("head_cent", [P, P])
        value_sum = sb("value_sum", [P, K, P])
        value_sel = sb("value_sel", [P, K, P], F32R)
        mean_w = sb("mean_w", [P, P])
        eps4 = sb("eps4", [P, 1])
        eps1 = sb("eps1", [P, 1])
        half_ln = sb("half_ln", [P, 2 * NC])

        x_in = sb("x_in", [P, 2 * NC, GT])
        diff = sb("diff", [P, NC, GT])
        summ = sb("summ", [P, NC, GT])
        th = sb("th_sq", [P, NC, GT])
        y_sq = th
        h2 = sb("h2", [P, NC, GT])
        h_res = sb("h_res", [P, 2, NC, GT])
        cent = sb("cent", [P, NC, GT])
        sq_xxx = sb("sq_xxx", [P, NC, GT])
        rstd = sb("rstd", [P, GT])
        xn = sb("xn", [P, NC, GB, T + 1])
        sx = sb("sx", [P, NC, GT])
        m_a = sb("m_a", [P, GT])
        m_b = sb("m_b", [LORA, GT])
        x_f = sb("x_f", [P, NMIX, NC, GT])
        x_f_flat = x_f[:].rearrange("p f c n -> p (f c n)")
        td_h = sb("td_h", [DW, GT])
        w_s = sb("w_s", [P, 2, NC, GB, T])
        k_s = sb("k_s", [P, 2, NC, GT])
        r_s = sb("r_s", [P, 2, NC, GB, T])
        v_f = sb("v_f", [P, NC, GT])
        v_p = [sb(f"v_p{n}", [P, 2, NC, GT], F32R) for n in range(2)]
        rk = sb("rk", [P, NC, GT])
        gate = sb("gate", [P, 2, NC, GT])
        y_now = sb("y_now", [P, 2, NC, GT])
        kv = sb("kv", [P, RING, GT])
        state = sb("state", [P, RING, GT + 1])
        rs = sb("rs", [P, RING, GT])
        y = sb("y", [P, NC, GT])
        rows = sb("rows", [P, GB, C])

        bank = [ps(f"front{n}", [P, 512]) for n in range(FRONT_BANKS)]
        tail_bank = ps("tail_bank", [P, 512])
        vrep = [ps(f"vrep{n}", [P, 512]) for n in range(2)]
        y_ps = [ps(f"y_ps{n}", [P, 512]) for n in range(NC)]

        w_ready = ready
        made = sem("made")
        front_filled = [sem(f"front_filled{n}") for n in range(FRONT_BANKS)]
        front_read = [sem(f"front_read{n}") for n in range(FRONT_BANKS)]
        tail_filled = sem("tail_filled")
        tail_read = sem("tail_read")
        x_loaded = sem("x_loaded")
        diff_ready = sem("diff_ready")
        summ_ready = sem("summ_ready")
        gated = sem("gated")
        h_ready = sem("h_ready")
        res_ready = sem("res_ready")
        squared = sem("squared")
        rstd_ready = sem("rstd_ready")
        xn_ready = sem("xn_ready")
        sx_ready = sem("sx_ready")
        xxx_ready = sem("xxx_ready")
        xf_ready = sem("xf_ready")
        decay_ready = sem("decay_ready")
        r_ready = sem("r_ready")
        tg_ready = sem("tg_ready")
        v_part = [sem(f"v_part{n}") for n in range(2)]
        vrep_ready = sem("vrep_ready")
        kv_ready = sem("kv_ready")
        scanned = sem("scanned")
        rs_ready = sem("rs_ready")
        y_part = sem("y_part")
        y_read = sem("y_read")
        ruk_filled = sem("ruk_filled")
        ruk_read = sem("ruk_read")
        y_squared = sem("y_squared")
        yrstd_ready = sem("yrstd_ready")
        yn_ready = sem("yn_ready")
        affine_ready = sem("affine_ready")
        z_ready = sem("z_ready")
        stored = sem("stored")

        x_dram = d["x"].rearrange("a (c p) n -> p (a c) n", p=P)
        out_dram = d["out"].rearrange("b t c -> t b c")

        def filled(eng, use, g):
            k = FRONT_INDEX[use]
            wait(eng, front_filled[k % FRONT_BANKS], g * FRONT_TURNS + (k // FRONT_BANKS + 1))

        def was_read(eng, use, g):
            k = FRONT_INDEX[use]
            wait(eng, front_read[k % FRONT_BANKS], g * FRONT_TURNS + (k // FRONT_BANKS + 1))

        def free(eng, use, g):
            k = FRONT_INDEX[use]
            wait(eng, front_read[k % FRONT_BANKS], g * FRONT_TURNS + k // FRONT_BANKS)

        def bank_of(use):
            return bank[FRONT_INDEX[use] % FRONT_BANKS]

        def fill_sem(use):
            return front_filled[FRONT_INDEX[use] % FRONT_BANKS]

        def read_sem(use):
            return front_read[FRONT_INDEX[use] % FRONT_BANKS]

        def by_seq(ap):
            return ap.rearrange("p (b t) -> p b t", b=GB)

        block = ctx.enter_context(nc.Block())

        @block.sync
        def _(sp):
            weights = [(w_tok, "tok_w"), (w_r, "Wr"), (w_k, "Wk"), (w_v, "Wv"), (w_g, "Wg"), (w_o, "Wo"),
                       (tm_w1, "tm_w1"), (td_w1, "td_w1")]

            def load(g):
                sp.dma_start(x_in[:], x_dram[:, :, bass.ds(g * GT, GT)]).then_inc(x_loaded, 16)

            load(0)
            for tile, name in weights:
                sp.dma_start(tile[:], d[name].rearrange("(c p) n -> p c n", p=P)).then_inc(w_ready, 16)
            sp.dma_start(tm_w2[:], d["tm_w2"][0:P, :]).then_inc(w_ready, 16)
            sp.dma_start(tm_w2_last[:], d["tm_w2"][P:P + LORA, :]).then_inc(w_ready, 16)
            sp.dma_start(td_w2[:], d["td_w2"]).then_inc(w_ready, 16)
            sp.dma_start(head_mean[:], d["head_block"]).then_inc(w_ready, 16)
            sp.dma_start(value_sum[:], d["value_sum"].rearrange("p (v q) -> p v q", v=K)).then_inc(w_ready, 16)
            sp.dma_start(x_f_flat[:, 0:K * P], d["value_sel"]).then_inc(w_ready, 16)

            def slot(u, scan, front, tail):
                if u == 0 and front is not None:
                    g, par, half = front
                    if not (isinstance(g, int) and g + 1 >= NG):
                        wait(sp, diff_ready, g + 1)
                        wait(sp, summ_ready, g + 1)
                        load(g + 1)
                if u == 14 and tail is not None:
                    g, par, half = tail
                    wait(sp, tail_read, g * TU + TU)
                    sp.dma_start(out_dram[:, bass.ds(g * GB, GB), :], rows[0:T]).then_inc(stored, 16)

            walk(sp, slot)
            sp.wait_ge(stored, 16 * NG)

        @block.tensor
        def _(pe):
            pe.wait_ge(w_ready, 16 * 16)
            pe.wait_ge(made, 13)

            def dense(use, g, weights, moving, m=P, cols=None):
                free(pe, use, g)
                for c in range(NC):
                    last = nc.tensor.matmul(bank_of(use)[0:m, 0:GT], weights(c), moving(c),
                                            start=(c == 0), stop=(c == NC - 1))
                last.then_inc(fill_sem(use), 1)

            def ysum(u, g):
                c, v = divmod(u, K)
                wait(pe, rs_ready, g * UNITS + u + 1)
                if v == 0:
                    wait(pe, y_read, g * NC + c - 1)
                nc.tensor.matmul(y_ps[c][:, 0:GT], value_sum[:, v, :], rs[:, u % RING, :], start=(v == 0),
                                 stop=(v == K - 1)).then_inc(y_part, 1)

            def slot(u, scan, front, tail):
                if scan is not None:
                    g, par, half = scan
                    c, v = divmod(u, K)
                    if u == 0:
                        wait(pe, v_part[1], g + 1)
                    wait(pe, kv_ready, g * UNITS + u - 1)
                    for n in range(2):
                        last = nc.tensor.matmul(vrep[u % 2][:, 0:GT], value_sel[:, v, :], v_p[n][:, par, c, :],
                                                start=(n == 0), stop=(n == 1))
                    last.then_inc(vrep_ready, 1)
                    if u >= 3:
                        ysum(u - 3, g)
                if u < 3 and tail is not None:
                    ysum(UNITS - 3 + u, tail[0])
                if front is not None:
                    g, par, half = front
                    for c in range(NC):
                        if u == SLOT[f"tok{c}"]:
                            if c == 0:
                                wait(pe, diff_ready, g + 1)
                            dense(f"tok{c}", g, lambda i: w_tok[:, i, c * P:(c + 1) * P], lambda i: diff[:, i, :])
                    if u == SLOT["mean"]:
                        wait(pe, h_ready, g + 1)
                        dense("mean", g, lambda c: mean_w[:], lambda c: h2[:, c, :])
                    if u == SLOT["var"]:
                        wait(pe, squared, g + 1)
                        dense("var", g, lambda c: mean_w[:], lambda c: sq_xxx[:, c, :])
                    if u == SLOT["m"]:
                        wait(pe, xxx_ready, g * NC + NC)
                        dense("m", g, lambda c: tm_w1[:, c, 0:P], lambda c: sq_xxx[:, c, :])
                    if u == SLOT["m4"]:
                        dense("m4", g, lambda c: tm_w1[:, c, P:P + LORA], lambda c: sq_xxx[:, c, :], m=LORA)
                    if SLOT["delta"] <= u < SLOT["delta"] + NMIX:
                        f = u - SLOT["delta"]
                        if f == 0:
                            was_read(pe, "m", g)
                        if f == NMIX - 1:
                            was_read(pe, "m4", g)
                        for c in range(NC):
                            use = f"delta{f}{c}"
                            free(pe, use, g)
                            cols = slice(c * P, (c + 1) * P)
                            if f < NMIX - 1:
                                part = slice(f * LORA, (f + 1) * LORA)
                                w2, m = tm_w2[part, cols], m_a[part, :]
                            else:
                                w2, m = tm_w2_last[:, cols], m_b[:]
                            nc.tensor.matmul(bank_of(use)[:, 0:GT], w2, m, start=True, stop=True) \
                                .then_inc(fill_sem(use), 1)
                    if u == SLOT["td"]:
                        wait(pe, xf_ready, g * NMIX + 1)
                        dense("td", g, lambda c: td_w1[:, c, :], lambda c: x_f[:, 0, c, :], m=DW)
                    if u == SLOT["ww"]:
                        was_read(pe, "td", g)
                        for c in range(NC):
                            use = f"ww{c}"
                            free(pe, use, g)
                            nc.tensor.matmul(bank_of(use)[:, 0:GT], td_w2[:, c * P:(c + 1) * P], td_h[:],
                                             start=True, stop=True).then_inc(fill_sem(use), 1)
                    for f, (name, weight) in enumerate((("k", w_k), ("v", w_v), ("r", w_r), ("g", w_g)), 1):
                        for c in range(NC):
                            if u == SLOT[f"{name}{c}"]:
                                wait(pe, xf_ready, g * NMIX + f + 1)
                                dense(f"{name}{c}", g, lambda i: weight[:, i, c * P:(c + 1) * P],
                                      lambda i: x_f[:, f, i, :])
                    for c in range(NC):
                        if u == SLOT[f"ruk{c}"]:
                            was_read(pe, f"r{c}", g)
                            if c == 0:
                                wait(pe, tail_read, g * TU - TU)
                            else:
                                wait(pe, ruk_read, g * NC + 1)
                            nc.tensor.matmul(tail_bank[:, 0:GT], head_u[:, c, :], rk[:, c, :], start=True,
                                             stop=True).then_inc(ruk_filled, 1)
                if tail is not None:
                    g, par, half = tail
                    if u in (4, 5):
                        c = u - 4
                        if c == 0:
                            last_front = (g + 1) * NC + NC
                            wait(pe, ruk_read, min(last_front, NG * NC) if isinstance(g, int) else last_front)
                            wait(pe, tail_read, g * TU)
                        else:
                            wait(pe, tail_read, g * TU + 1)
                        wait(pe, y_read, g * NC + c + 1)
                        nc.tensor.matmul(tail_bank[:, 0:GT], head_cent[:], y[:, c, :], start=True, stop=True) \
                            .then_inc(tail_filled, 1)
                    if u in (6, 7):
                        c = u - 6
                        wait(pe, tail_read, g * TU + 2 + c)
                        wait(pe, y_squared, g * NC + c + 1)
                        nc.tensor.matmul(tail_bank[:, 0:GT], head_mean[:], y_sq[:, c, :], start=True, stop=True) \
                            .then_inc(tail_filled, 1)
                    if u in (11, 12):
                        j = u - 11
                        if j == 0:
                            wait(pe, z_ready, g + 1)
                            wait(pe, res_ready, g + 1)
                        wait(pe, tail_read, g * TU + 4 + j)
                        for b in range(2):
                            seq = slice((2 * j + b) * T, (2 * j + b + 1) * T)
                            for c in range(NC):
                                nc.tensor.matmul(tail_bank[0:T, b * C:(b + 1) * C], y[:, c, seq], w_o[:, c, :],
                                                 start=(c == 0), stop=False, skip_group_check=True)
                            for c in range(NC):
                                at = b * C + c * P
                                last = nc.tensor.matmul(tail_bank[0:T, at:at + P], h_res[:, par, c, seq], ident[:],
                                                        start=False, stop=(c == NC - 1), skip_group_check=True)
                        last.then_inc(tail_filled, 1)

            walk(pe, slot)

        @block.vector
        def _(dve):
            nc.vector.memset(mean_w[:], 1.0 / C).then_inc(made, 1)
            nc.vector.memset(eps4[:], 4 * EPS).then_inc(made, 1)
            nc.vector.memset(eps1[:], EPS).then_inc(made, 1)
            nc.vector.memset(w_s[:], 0.0).then_inc(made, 1)
            nc.vector.memset(r_s[:], 0.0).then_inc(made, 1)
            nc.vector.memset(state[:], 0.0).then_inc(made, 1)
            nc.vector.memset(xn[:], 0.0).then_inc(made, 1)
            dve.wait_ge(w_ready, 16 * 16)
            nc.vector.tensor_copy(value_sel[:], x_f_flat[:, 0:K * P].rearrange("p (v q) -> p v q", v=K)) \
                .then_inc(made, 1)
            for c in range(NC):
                u_col = params[:, COL["u"] + c:COL["u"] + c + 1]
                nc.vector.tensor_scalar(head_u[:, c, :], head_mean[:], u_col, None, ALU.mult).then_inc(made, 1)
            dve.wait_ge(made, 10)
            nc.vector.tensor_scalar(head_mean[:], head_mean[:], 1.0 / K, None, ALU.mult).then_inc(made, 1)
            dve.wait_ge(made, 11)
            nc.vector.tensor_tensor(head_cent[:], ident[:], head_mean[:], ALU.subtract).then_inc(made, 1)
            nc.vector.tensor_scalar(half_ln[:], params[:, COL["ln_w"]:COL["ln_w"] + 2 * NC], 0.5, None,
                                    ALU.mult).then_inc(made, 1)
            dve.wait_ge(made, 13)

            def scan_unit(u, g, par):
                c = u // K
                if u == 0:
                    wait(dve, decay_ready, g * NC + NC)
                wait(dve, kv_ready, g * UNITS + u + 1)
                wait(dve, rs_ready, g * UNITS + u + 1 - RING)
                nc.vector.tensor_tensor_scan(state[:, u % RING, 1:GT + 1],
                                             w_s[:, par, c].rearrange("p b t -> p (b t)"), kv[:, u % RING, :],
                                             0.0, ALU.mult, ALU.add).then_inc(scanned, 1)

            def take_y(c, group):
                g, par, half = group
                wait(dve, y_part, g * UNITS + (c + 1) * K)
                wait(dve, ruk_read, g * NC + c + 1)
                wait(dve, tail_filled, g * TU)
                nc.vector.tensor_tensor(y[:, c, :], y_ps[c][:, 0:GT], y_now[:, par, c, :], ALU.add) \
                    .then_inc(y_read, 1)

            def slot(u, scan, front, tail):
                if scan is not None:
                    g, par, half = scan
                    c = u // K
                    if u == 0:
                        was_read(dve, "k0", g)
                        was_read(dve, "k1", g)
                    wait(dve, vrep_ready, g * UNITS + u + 1)
                    wait(dve, scanned, g * UNITS + u + 1 - RING)
                    nc.vector.tensor_tensor(kv[:, u % RING, :], vrep[u % 2][:, 0:GT], k_s[:, par, c, :],
                                            ALU.mult).then_inc(kv_ready, 1)
                    if u >= 1:
                        scan_unit(u - 1, g, par)
                if u == 0 and tail is not None:
                    scan_unit(UNITS - 1, tail[0], tail[1])
                if u == 20 and scan is not None:
                    take_y(0, scan)
                if u == 3 and tail is not None:
                    take_y(1, tail)
                if front is not None:
                    g, par, half = front
                    if u == 3:
                        was_read(dve, "tok0", g)
                        was_read(dve, "tok1", g)
                        nc.vector.tensor_tensor(th[:], th[:], diff[:], ALU.mult).then_inc(gated, 1)
                    if u == 4:
                        wait(dve, gated, g + 1)
                        wait(dve, summ_ready, g + 1)
                        wait(dve, res_ready, g)
                        nc.vector.tensor_tensor(h2[:], th[:], summ[:], ALU.add).then_inc(h_ready, 1)
                    if u == 6:
                        filled(dve, "mean", g)
                        mean = bank_of("mean")[:, 0:GT].unsqueeze(1).to_broadcast([P, NC, GT])
                        nc.vector.tensor_tensor(cent[:], h2[:], mean, ALU.subtract).then_inc(read_sem("mean"), 1)
                    if u == 8:
                        wait(dve, rstd_ready, g + 1)
                        wait(dve, xf_ready, g * NMIX)
                        for c in range(NC):
                            last = nc.vector.tensor_tensor(xn[:, c, :, 1:T + 1], by_seq(cent[:, c, :]),
                                                           by_seq(rstd[:]), ALU.mult)
                        last.then_inc(xn_ready, 1)
                    if u == 11:
                        wait(dve, sx_ready, g + 1)
                        for c in range(NC):
                            maa_x = params[:, COL["maa_x"] + c:COL["maa_x"] + c + 1]
                            nc.vector.scalar_tensor_tensor(by_seq(sq_xxx[:, c, :]), by_seq(sx[:, c, :]), maa_x,
                                                           xn[:, c, :, 1:T + 1], ALU.mult, ALU.add) \
                                .then_inc(xxx_ready, 1)
                    if 15 <= u < 15 + NMIX:
                        f = u - 15
                        for c in range(NC):
                            use = f"delta{f}{c}"
                            maa = params[:, COL["maa"] + f * NC + c:COL["maa"] + f * NC + c + 1]
                            filled(dve, use, g)
                            nc.vector.scalar_tensor_tensor(x_f[:, f, c, :], bank_of(use)[:, 0:GT], maa,
                                                           sx[:, c, :], ALU.add, ALU.mult) \
                                .then_inc(read_sem(use), 1)
                    for c in range(NC):
                        use = f"r{c}"
                        if u == SLOT[use] + 1:
                            was_read(dve, f"k{c}", g)
                            wait(dve, r_ready, g * NC + c + 1)
                            nc.vector.tensor_tensor(rk[:, c, :], bank_of(use)[:, 0:GT], k_s[:, par, c, :],
                                                    ALU.mult).then_inc(read_sem(use), 1)
                    for c in range(NC):
                        use = f"g{c}"
                        if u == SLOT[use] + 1:
                            wait(dve, tg_ready, g * NC + c + 1)
                            nc.vector.scalar_tensor_tensor(gate[:, par, c, :], gate[:, par, c, :], 1.0,
                                                           bank_of(use)[:, 0:GT], ALU.add, ALU.mult) \
                                .then_inc(read_sem(use), 1)
                    for c in range(NC):
                        if u == SLOT[f"ruk{c}"] + 1:
                            wait(dve, ruk_filled, g * NC + c + 1)
                            nc.vector.tensor_tensor(y_now[:, par, c, :], tail_bank[:, 0:GT], v_f[:, c, :],
                                                    ALU.mult).then_inc(ruk_read, 1)
                if tail is not None:
                    g, par, half = tail
                    if u == 8:
                        wait(dve, yrstd_ready, g + 1)
                        wait(dve, tail_read, g * TU + 2)
                        nc.vector.tensor_tensor(y[:], y[:], y_sq[:], ALU.mult).then_inc(yn_ready, 1)

            walk(dve, slot)

        @block.gpsimd
        def _(pool):
            pool.wait_ge(made, 13)

            def rs_unit(u, g, par):
                wait(pool, scanned, g * UNITS + u + 1)
                if u == 0:
                    wait(pool, r_ready, g * NC + NC)
                wait(pool, y_part, g * UNITS + u + 1 - RING)
                nc.gpsimd.tensor_tensor(rs[:, u % RING, :], r_s[:, par, u // K].rearrange("p b t -> p (b t)"),
                                        state[:, u % RING, 0:GT], ALU.mult).then_inc(rs_ready, 1)

            def slot(u, scan, front, tail):
                if scan is not None and u >= 2:
                    rs_unit(u - 2, scan[0], scan[1])
                if u < 2 and tail is not None:
                    rs_unit(UNITS - 2 + u, tail[0], tail[1])
                if front is not None:
                    g, par, half = front
                    if u == 0:
                        wait(pool, x_loaded, g * 16 + 16)
                        wait(pool, h_ready, g)
                        nc.gpsimd.tensor_tensor(diff[:], x_in[:, 0:NC], x_in[:, NC:2 * NC],
                                                ALU.subtract).then_inc(diff_ready, 1)
                        nc.gpsimd.tensor_tensor(summ[:], x_in[:, 0:NC], x_in[:, NC:2 * NC],
                                                ALU.add).then_inc(summ_ready, 1)
                    if u == 9:
                        wait(pool, xn_ready, g + 1)
                        for c in range(NC):
                            last = nc.gpsimd.tensor_tensor(by_seq(sx[:, c, :]), xn[:, c, :, 0:T],
                                                           xn[:, c, :, 1:T + 1], ALU.subtract)
                        last.then_inc(sx_ready, 1)
                    if 16 <= u < 16 + NMIX:
                        f = u - 16
                        was_read(pool, f"delta{f}0", g)
                        was_read(pool, f"delta{f}1", g)
                        for c in range(NC):
                            last = nc.gpsimd.tensor_tensor(by_seq(x_f[:, f, c, :]), by_seq(x_f[:, f, c, :]),
                                                           xn[:, c, :, 1:T + 1], ALU.add)
                        last.then_inc(xf_ready, 1)
                    if u == 22:
                        wait(pool, v_part[0], g + 1)
                        nc.gpsimd.tensor_tensor(v_p[1][:, par], v_f[:], v_p[0][:, par].bitcast(F32), ALU.subtract) \
                            .then_inc(v_part[1], 1)
                if tail is not None:
                    g, par, half = tail
                    if u == 10:
                        wait(pool, affine_ready, g + 1)
                        nc.gpsimd.tensor_tensor(y[:], y[:], gate[:, par], ALU.mult).then_inc(z_ready, 1)

            walk(pool, slot)

        @block.scalar
        def _(act):
            act.wait_ge(w_ready, 16 * 16)
            act.wait_ge(made, 13)

            def column(name, c):
                return params[:, COL[name] + c:COL[name] + c + 1]

            def slot(u, scan, front, tail):
                if front is not None:
                    g, par, half = front
                    for c in range(NC):
                        use = f"tok{c}"
                        if u == SLOT[use]:
                            wait(act, h_ready, g)
                            filled(act, use, g)
                            nc.scalar.activation(th[:, c, :], bank_of(use)[:, 0:GT], ACT.Tanh, scale=0.5) \
                                .then_inc(read_sem(use), 1)
                    if u == 6:
                        was_read(act, "mean", g)
                        nc.scalar.activation(sq_xxx[:], cent[:], ACT.Square).then_inc(squared, 1)
                    if u == 7:
                        filled(act, "var", g)
                        wait(act, xn_ready, g)
                        nc.scalar.activation(rstd[:], bank_of("var")[:, 0:GT], ACT.Ln, bias=eps4[:]) \
                            .then_inc(read_sem("var"), 1)
                        was_read(act, "var", g)
                        nc.scalar.activation(rstd[:], rstd[:], ACT.Exp, scale=-0.5).then_inc(rstd_ready, 1)
                    if u == SLOT["m4"]:
                        filled(act, "m", g)
                        nc.scalar.activation(m_a[:], bank_of("m")[:, 0:GT], ACT.Tanh).then_inc(read_sem("m"), 1)
                        filled(act, "m4", g)
                        nc.scalar.activation(m_b[:], bank_of("m4")[0:LORA, 0:GT], ACT.Tanh) \
                            .then_inc(read_sem("m4"), 1)
                    if u == SLOT["td"]:
                        filled(act, "td", g)
                        nc.scalar.activation(td_h[:], bank_of("td")[0:DW, 0:GT], ACT.Tanh) \
                            .then_inc(read_sem("td"), 1)
                    if u == SLOT["ww"]:
                        wait(act, scanned, g * UNITS - UNITS)
                        for c in range(NC):
                            use = f"ww{c}"
                            filled(act, use, g)
                            nc.scalar.activation(w_s[:, par, c, :, 1:T], by_seq(bank_of(use)[:, 0:GT])[:, :, 1:T],
                                                 ACT.Exp, bias=column("decay", c)).then_inc(read_sem(use), 1)
                        for c in range(NC):
                            was_read(act, f"ww{c}", g)
                            nc.scalar.activation(w_s[:, par, c, :, 1:T], w_s[:, par, c, :, 1:T], ACT.Exp,
                                                 scale=-1.0).then_inc(decay_ready, 1)
                    for c in range(NC):
                        use = f"k{c}"
                        if u == SLOT[use]:
                            wait(act, kv_ready, g * UNITS - UNITS)
                            filled(act, use, g)
                            nc.scalar.copy(k_s[:, par, c, :], bank_of(use)[:, 0:GT]).then_inc(read_sem(use), 1)
                    if u == SLOT["v1"]:
                        wait(act, v_part[1], g)
                        wait(act, ruk_read, g * NC)
                        for c in range(NC):
                            use = f"v{c}"
                            filled(act, use, g)
                            nc.scalar.copy(v_f[:, c, :], bank_of(use)[:, 0:GT]).then_inc(read_sem(use), 1)
                        was_read(act, "v0", g)
                        was_read(act, "v1", g)
                        wait(act, vrep_ready, g * UNITS - UNITS)
                        nc.scalar.copy(v_p[0][:, par], v_f[:]).then_inc(v_part[0], 1)
                    for c in range(NC):
                        use = f"r{c}"
                        if u == SLOT[use]:
                            wait(act, rs_ready, g * UNITS - UNITS)
                            filled(act, use, g)
                            nc.scalar.copy(r_s[:, par, c, :, 1:T], by_seq(bank_of(use)[:, 0:GT])[:, :, 1:T]) \
                                .then_inc(r_ready, 1)
                    for c in range(NC):
                        use = f"g{c}"
                        if u == SLOT[use]:
                            wait(act, z_ready, g - 1)
                            filled(act, use, g)
                            nc.scalar.activation(gate[:, par, c, :], bank_of(use)[:, 0:GT], ACT.Tanh, scale=0.5) \
                                .then_inc(tg_ready, 1)
                    if u == 18:
                        wait(act, tail_filled, g * TU - TU)
                        nc.scalar.mul(h_res[:, par], h2[:], 0.5).then_inc(res_ready, 1)
                if tail is not None:
                    g, par, half = tail
                    if u in (4, 5):
                        c = u - 4
                        if c == 0:
                            wait(act, h_ready, min(g + 3, NG) if isinstance(g, int) else g + 3)
                        wait(act, tail_filled, g * TU + c + 1)
                        nc.scalar.activation(y_sq[:, c, :], tail_bank[:, 0:GT], ACT.Square).then_inc(y_squared, 1)
                        nc.scalar.copy(y[:, c, :], tail_bank[:, 0:GT]).then_inc(tail_read, 1)
                    if u == 7:
                        for c in range(NC):
                            wait(act, tail_filled, g * TU + 3 + c)
                            nc.scalar.activation(y_sq[:, c, :], tail_bank[:, 0:GT], ACT.Ln, bias=eps1[:]) \
                                .then_inc(tail_read, 1)
                        wait(act, tail_read, g * TU + 4)
                        nc.scalar.activation(y_sq[:], y_sq[:], ACT.Exp, scale=-0.5).then_inc(yrstd_ready, 1)
                    if u == 9:
                        wait(act, yn_ready, g + 1)
                        for c in range(NC):
                            last = nc.scalar.activation(y[:, c, :], y[:, c, :], ACT.Identity,
                                                        bias=half_ln[:, NC + c:NC + c + 1],
                                                        scale=half_ln[:, c:c + 1])
                        last.then_inc(affine_ready, 1)
                    if u in (12, 13):
                        j = u - 12
                        wait(act, tail_filled, g * TU + j + 5)
                        if j == 0:
                            wait(act, stored, g * 16)
                        nc.scalar.copy(rows[0:T, 2 * j:2 * j + 2, :],
                                       tail_bank[0:T, :].rearrange("p (b c) -> p b c", b=2)) \
                            .then_inc(tail_read, 1)

            walk(act, slot)


def expert_phase(nc, d, const):
    ident, params, ready = const
    with ExitStack() as ctx:
        def sb(name, shape, dt=F32):
            return ctx.enter_context(nc.sbuf_tensor(name, shape, dt))

        def ps(name, shape):
            return ctx.enter_context(nc.psum_tensor(name, shape, F32))

        def sem(name):
            return ctx.enter_context(nc.semaphore(name))

        idx = sb("idx", [P, NT], I32)
        idx_f = sb("idx_f", [P, NT])
        spare = sb("spare", [P, 1])
        earlier = sb("earlier", [P, P])
        ones_row = sb("ones_row", [1, P])
        b1 = sb("b1", [P, E, NF])
        b2 = sb("b2", [1, E, C])
        w1 = sb("w1", [P, 2, NC, FF])
        w2 = sb("w2", [P, 2, NF, C])
        got = sb("got", [P, NT, C])
        got_w = sb("got_w", [P, NT, E])
        stats = sb("stats", [P, NT, 6])
        moments = sb("moments", [P, NT, 2])
        rstd = sb("rstd2", [P, NT])
        normed = sb("normed", [P, 2, C])
        xT = sb("xT", [P, 2, NC, CAP])
        hid = sb("hid", [P, NF, CAP])
        weighted = sb("weighted", [P, 2, C])
        same = sb("same", [P, 2, P])
        same_before = sb("same_before", [P, P])
        dups = sb("dups", [P, NT])
        target_f = sb("target_f", [P, NT])
        shift_f = sb("shift_f", [P, NT])
        target = sb("target", [P, NT], I32)
        summed = sb("summed", [P, 2, C])
        zero = sb("zero", [P, C])

        t_ps = [ps(f"t_ps{n}", [P, 512]) for n in range(2)]
        h_ps = [ps(f"h_ps{n}", [P, 512]) for n in range(2)]
        o_ps = [ps(f"o_ps{n}", [P, 512]) for n in range(2)]
        i_ps = ps("i_ps", [P, 512])
        s_ps = ps("s_ps", [P, 512])

        loaded = sem("e_loaded")
        w_loaded = [sem(f"e_w_loaded{n}") for n in range(2)]
        table_ready = sem("table_ready")
        gathered = sem("gathered")
        made = sem("e_made")
        zero_ready = sem("zero_ready")
        root_ready = sem("root_ready")
        stats_ready = sem("stats_ready")
        moments_ready = sem("moments_ready")
        var_ready = sem("e_var_ready")
        rstd_ready = sem("e_rstd_ready")
        normed_ready = sem("normed_ready")
        turned = sem("turned")
        xT_ready = sem("xT_ready")
        h_filled = sem("h_filled")
        h_read = sem("h_read")
        o_filled = sem("o_filled")
        weighted_ready = sem("weighted_ready")
        i_filled = sem("i_filled")
        same_ready = sem("same_ready")
        before_ready = sem("before_ready")
        dups_ready = sem("dups_ready")
        target_step = sem("target_step")
        s_filled = sem("s_filled")
        summed_ready = sem("summed_ready")
        scattered = sem("scattered")
        copied = sem("copied")

        out_rows = d["out"].rearrange("b t c -> (b t) c")
        table = d["table"]
        weight_rows = d["combine_weights"]
        w1_dram = d["W1"].rearrange("e (c p) f -> e p c f", p=P)
        w2_dram = d["W2"].rearrange("e (n p) c -> e p n c", p=P)

        block = ctx.enter_context(nc.Block())

        @block.sync
        def _(sp):
            sp.dma_start(idx[:], d["idx"]).then_inc(loaded, 16)
            sp.dma_start(spare[:], d["spare"]).then_inc(loaded, 16)
            sp.dma_start(earlier[:], d["earlier"]).then_inc(loaded, 16)
            sp.dma_start(b1[:], d["b1"].rearrange("p (e n) -> p e n", e=E)).then_inc(loaded, 16)
            sp.dma_start(b2[:], d["b2"].rearrange("(a e) c -> a e c", a=1)).then_inc(loaded, 16)
            sp.dma_start(table[0:NTOK, :], out_rows[0:NTOK, :]).then_inc(table_ready, 16)
            sp.wait_ge(zero_ready, 1)
            sp.dma_start(table[NTOK:TABLE, :], zero[:]).then_inc(table_ready, 16)
            for e in range(E):
                if e >= 2:
                    sp.wait_ge(o_filled, TPE * (e - 1))
                sp.dma_start(w1[:, e % 2], w1_dram[e]).then_inc(w_loaded[e % 2], 16)
                sp.dma_start(w2[:, e % 2], w2_dram[e]).then_inc(w_loaded[e % 2], 16)
            sp.wait_ge(scattered, 16 * NT)
            sp.dma_start(out_rows[0:NTOK, :], table[0:NTOK, :]).then_inc(copied, 16)
            sp.wait_ge(copied, 16)

        @block.gpsimd
        def _(pool):
            nc.gpsimd.memset(zero[:], 0.0).then_inc(zero_ready, 1)
            pool.wait_ge(loaded, 16 * 5)
            for t in range(NT):
                at = bass.IndirectOffsetOnAxis(ap=idx[:, t:t + 1], axis=0)
                nc.gpsimd.indirect_dma_start(out=got[:, t, :], out_offset=None, in_=out_rows[:],
                                             in_offset=at).then_inc(gathered, 16)
                nc.gpsimd.indirect_dma_start(out=got_w[:, t, :], out_offset=None, in_=weight_rows[:],
                                             in_offset=at).then_inc(gathered, 16)
            pool.wait_ge(table_ready, 32)
            pool.wait_ge(target_step, 4)
            for t in range(NT):
                pool.wait_ge(summed_ready, t + 1)
                if t >= 1:
                    pool.wait_ge(scattered, 16 * t)
                nc.gpsimd.indirect_dma_start(
                    out=table[:], out_offset=bass.IndirectOffsetOnAxis(ap=target[:, t:t + 1], axis=0),
                    in_=summed[:, t % 2, :], in_offset=None, compute_op=ALU.add).then_inc(scattered, 16)

        @block.vector
        def _(dve):
            nc.vector.memset(ones_row[:], 1.0).then_inc(made, 1)
            dve.wait_ge(loaded, 16 * 5)
            nc.vector.tensor_copy(idx_f[:], idx[:]).then_inc(made, 1)
            dve.wait_ge(made, 2)
            for t in range(NT):
                dve.wait_ge(i_filled, t + 1)
                if t >= 1:
                    dve.wait_ge(dups_ready, t)
                nc.vector.scalar_tensor_tensor(same_before[:], i_ps[:, 0:P],
                                               idx_f[:, t:t + 1], earlier[:], ALU.is_equal, ALU.mult) \
                    .then_inc(before_ready, 1)
                dve.wait_ge(before_ready, t + 1)
                nc.vector.tensor_reduce(dups[:, t:t + 1], same_before[:], AX_X, ALU.max).then_inc(dups_ready, 1)
            dve.wait_ge(dups_ready, NT)
            nc.vector.tensor_scalar(shift_f[:], idx_f[:], spare[:, 0:1], -1.0, ALU.subtract, ALU.mult) \
                .then_inc(target_step, 1)
            dve.wait_ge(target_step, 1)
            nc.vector.tensor_tensor(shift_f[:], shift_f[:], dups[:], ALU.mult).then_inc(target_step, 1)
            dve.wait_ge(target_step, 2)
            nc.vector.tensor_tensor(target_f[:], shift_f[:], idx_f[:], ALU.add).then_inc(target_step, 1)
            dve.wait_ge(target_step, 3)
            nc.vector.tensor_copy(target[:], target_f[:]).then_inc(target_step, 1)
            dve.wait_ge(gathered, 32 * NT)
            for t in range(NT):
                nc.vector.bn_stats(stats[:, t, :], got[:, t, :]).then_inc(stats_ready, 1)
            for t in range(NT):
                dve.wait_ge(stats_ready, t + 1)
                nc.vector.bn_aggr(moments[:, t, :], stats[:, t, :]).then_inc(moments_ready, 1)
            dve.wait_ge(moments_ready, NT)
            nc.vector.tensor_scalar(rstd[:], moments[:, :, 1], EPS, None, ALU.add).then_inc(var_ready, 1)
            dve.wait_ge(root_ready, 1)
            nc.vector.reciprocal(rstd[:], rstd[:]).then_inc(rstd_ready, 1)
            dve.wait_ge(rstd_ready, 1)

            def normalise(t):
                if t >= 2:
                    dve.wait_ge(turned, t - 1)
                nc.vector.tensor_scalar(normed[:, t % 2, :], got[:, t, :], moments[:, t, 0:1], rstd[:, t:t + 1],
                                        ALU.subtract, ALU.mult).then_inc(normed_ready, 1)

            def collect(t):
                if t >= 2:
                    dve.wait_ge(s_filled, t - 1)
                nc.vector.tensor_scalar(same[:, t % 2, :], i_ps[:, 0:P],
                                        idx_f[:, t:t + 1], None, ALU.is_equal).then_inc(same_ready, 1)

            def take(t):
                dve.wait_ge(s_filled, t + 1)
                if t >= 2:
                    dve.wait_ge(scattered, 16 * (t - 1))
                nc.vector.tensor_copy(summed[:, t % 2, :], s_ps[:, 0:C]).then_inc(summed_ready, 1)

            for e in range(E):
                if e == 0:
                    for t in range(TPE):
                        normalise(t)
                if e + 1 < E:
                    for j in range(TPE):
                        normalise((e + 1) * TPE + j)
                for j in range(TPE):
                    t = e * TPE + j
                    dve.wait_ge(i_filled, NT + t + 1)
                    collect(t)
                    take(t)

        @block.tensor
        def _(pe):
            pe.wait_ge(made, 2)

            def turn_index(t):
                nc.tensor.transpose(i_ps[:, 0:P], idx_f[:, t:t + 1].to_broadcast([P, P]),
                                    ident[:]).then_inc(i_filled, 1)

            def turn_rows(e):
                for j in range(TPE):
                    t = e * TPE + j
                    pe.wait_ge(normed_ready, t + 1)
                    if j == 0 and e >= 1:
                        pe.wait_ge(xT_ready, NC * e)
                    for c in range(NC):
                        last = nc.tensor.transpose(t_ps[c][:, j * P:(j + 1) * P], normed[:, t % 2, c * P:(c + 1) * P],
                                                   ident[:])
                    last.then_inc(turned, 1)

            for t in range(NT):
                if t >= 1:
                    pe.wait_ge(before_ready, t)
                turn_index(t)
            turn_rows(0)
            for e in range(E):
                pe.wait_ge(xT_ready, NC * (e + 1))
                pe.wait_ge(w_loaded[e % 2], 32 * (e // 2 + 1))
                for n in range(NF):
                    q = e * NF + n
                    if q >= 2:
                        pe.wait_ge(h_read, q - 1)
                    for c in range(NC):
                        last = nc.tensor.matmul(h_ps[q % 2][:], w1[:, e % 2, c, n * P:(n + 1) * P],
                                                xT[:, e % 2, c, :], start=(c == 0), stop=(c == NC - 1))
                    last.then_inc(h_filled, 1)
                if e >= 1:
                    sum_same(nc, pe, e * TPE - 1, same, weighted, s_ps, same_ready, weighted_ready, summed_ready, s_filled)
                if e + 1 < E:
                    turn_rows(e + 1)
                pe.wait_ge(h_read, NF * (e + 1))
                for j in range(TPE):
                    t = e * TPE + j
                    if t >= 2:
                        pe.wait_ge(weighted_ready, t - 1)
                    nc.tensor.matmul(o_ps[t % 2][:, 0:C], ones_row[:], b2[:, e, :], start=True, stop=False)
                    for n in range(NF):
                        last = nc.tensor.matmul(o_ps[t % 2][:, 0:C], hid[:, n, j * P:(j + 1) * P], w2[:, e % 2, n, :],
                                                start=False, stop=(n == NF - 1))
                    last.then_inc(o_filled, 1)
                    if t >= 1:
                        pe.wait_ge(same_ready, t)
                    else:
                        pe.wait_ge(dups_ready, NT)
                    turn_index(t)
                    if j >= 1:
                        sum_same(nc, pe, t - 1, same, weighted, s_ps, same_ready, weighted_ready, summed_ready, s_filled)
            sum_same(nc, pe, NT - 1, same, weighted, s_ps, same_ready, weighted_ready, summed_ready, s_filled)

        @block.scalar
        def _(act):
            def take_turned(e):
                act.wait_ge(turned, TPE * (e + 1))
                if e >= 2:
                    act.wait_ge(h_filled, NF * (e - 1))
                for c in range(NC):
                    nc.scalar.copy(xT[:, e % 2, c, :], t_ps[c][:]).then_inc(xT_ready, 1)

            act.wait_ge(loaded, 16 * 5)
            act.wait_ge(gathered, 32 * NT)
            act.wait_ge(var_ready, 1)
            nc.scalar.activation(rstd[:], rstd[:], ACT.Sqrt).then_inc(root_ready, 1)
            take_turned(0)
            for e in range(E):
                if e >= 1:
                    act.wait_ge(o_filled, TPE * e)
                for n in range(NF):
                    q = e * NF + n
                    act.wait_ge(h_filled, q + 1)
                    nc.scalar.activation(hid[:, n, :], h_ps[q % 2][:], ACT.Gelu_apprx_tanh,
                                         bias=b1[:, e, n:n + 1]).then_inc(h_read, 1)
                if e + 1 < E:
                    take_turned(e + 1)
                for j in range(TPE):
                    t = e * TPE + j
                    act.wait_ge(o_filled, t + 1)
                    if t >= 2:
                        act.wait_ge(s_filled, t - 1)
                    nc.scalar.activation(weighted[:, t % 2, :], o_ps[t % 2][:, 0:C], ACT.Copy,
                                         scale=got_w[:, t, e:e + 1]).then_inc(weighted_ready, 1)


def sum_same(nc, pe, t, same, weighted, s_ps, same_ready, weighted_ready, summed_ready, s_filled):
    pe.wait_ge(same_ready, t + 1)
    pe.wait_ge(weighted_ready, t + 1)
    if t >= 1:
        pe.wait_ge(summed_ready, t)
    nc.tensor.matmul(s_ps[:, 0:C], same[:, t % 2, :], weighted[:, t % 2, :], start=True, stop=True) \
        .then_inc(s_filled, 1)


def build(nc, d):
    with ExitStack() as ctx:
        ident = ctx.enter_context(nc.sbuf_tensor("ident", [P, P], F32))
        params = ctx.enter_context(nc.sbuf_tensor("params", [P, NPAR], F32))
        ready = ctx.enter_context(nc.semaphore("w_ready"))
        with nc.Block() as block:
            @block.sync
            def _(sp):
                sp.dma_start(ident[:], d["ident"]).then_inc(ready, 16)
                sp.dma_start(params[:], d["params"]).then_inc(ready, 16)
        attention_phase(nc, d, (ident, params, ready))
        expert_phase(nc, d, (ident, params, ready))


def kernel(**inputs):
    import numpy as np
    import concourse.bacc as bacc
    from concourse.bass_utils import run_bass_kernel_spmd

    def get(name):
        return np.asarray(inputs[name])

    def columns(a):
        return a.reshape(-1, P).T

    attn = "L0_attn_"
    idx = get("L0_ffn_top_idx")
    if idx.dtype.itemsize == 8:
        idx = np.ascontiguousarray(idx).view(np.int32).reshape(CAP, E, 2)[:, :, 0]
    own = np.arange(P)
    arrays = {
        "x": get("x").reshape(B * T, 2, C).transpose(1, 2, 0),
        "tok_w": get("L0_tok_w"), "Wr": get(attn + "Wr"), "Wk": get(attn + "Wk"), "Wv": get(attn + "Wv"),
        "Wg": get(attn + "Wg"), "Wo": get(attn + "Wo"), "tm_w1": get(attn + "tm_w1"),
        "tm_w2": get(attn + "tm_w2").reshape(NMIX * LORA, C), "td_w1": get(attn + "td_w1"),
        "td_w2": get(attn + "td_w2"),
        "params": np.concatenate([columns(get(attn + n)) for n in
                                  ("time_maa_x", "time_maa_wkvrg", "time_decay", "time_faaaa", "ln_w", "ln_b")], 1),
        "ident": np.eye(P, dtype=np.float32),
        "head_block": (own[:, None] // K == own // K).astype(np.float32),
        "value_sum": ((own[:, None, None] // K == own // K)
                      & (own % K == np.arange(K)[:, None])).astype(np.float32).reshape(P, -1),
        "value_sel": ((own[:, None, None] // K == own // K)
                      & (own[:, None, None] % K == np.arange(K)[:, None])).astype(np.float32).reshape(P, -1),
        "idx": idx.reshape(TPE, P, E).transpose(1, 2, 0).reshape(P, NT),
        "spare": (NTOK + own[:, None]).astype(np.float32),
        "earlier": (own < own[:, None]).astype(np.float32),
        "b1": get("L0_ffn_b1").reshape(E, NF, P).transpose(2, 0, 1).reshape(P, E * NF),
        "b2": get("L0_ffn_b2"), "W1": get("L0_ffn_W1"), "W2": get("L0_ffn_W2"),
        "combine_weights": get("L0_ffn_combine_weights"),
    }
    arrays = {"in_" + name: np.ascontiguousarray(a) for name, a in arrays.items()}
    nc = bacc.Bacc("TRN2", target_bir_lowering=False, num_devices=1)
    d = {name[3:]: nc.dram_tensor(name, a.shape, mybir.dt.from_np(a.dtype), kind="ExternalInput").ap()
         for name, a in arrays.items()}
    d["out"] = nc.dram_tensor("out", (B, T, C), F32, kind="ExternalOutput").ap()
    d["table"] = nc.dram_tensor("table", (TABLE, C), F32, kind="Internal").ap()
    build(nc, d)
    r = run_bass_kernel_spmd(nc, [arrays], core_ids=[0])
    return r.results[0]["out"]
```

```python
from contextlib import ExitStack

import concourse.bass as bass
from concourse import mybir

F32 = mybir.dt.float32
F32R = mybir.dt.float32r
I32 = mybir.dt.int32
ALU = mybir.AluOpType
ACT = mybir.ActivationFunctionType
AX_X = mybir.AxisListType.X

P = 128
C = 256
NC = C // P
T = 125
B = 128
GB = 4
GT = GB * T
NG = B // GB
H, K = 16, 16
LORA = 32
NMIX = 5
DW = 64
UNITS = NC * K
RING = 4
assert UNITS % RING == 0
EPS = 1e-5
E, CAP, FF, NTOK = 8, 512, 1024, 2048
NF = FF // P
TPE = CAP // P
NT = E * TPE
AHEAD = 3
TABLE = NTOK + P

COL = {"maa_x": 0, "maa": NC, "decay": NC * 6, "u": NC * 7, "ln_w": NC * 8, "ln_b": NC * 9}
NPAR = NC * 10

HI_LAG, LO_LAG, YLAG = 3, 5, 6
WHOLE = (1, 4, 5, 6, 24, 26, 27, 29, 30, 31)
SPLITS = UNITS - len(WHOLE)

FRONT_USES = (["tok0", "tok1", "mean", "var", "g0", "g1", "m", "m4"]
              + [f"delta{f}{c}" for f in range(NMIX) for c in range(NC)]
              + ["td", "v0", "v1", "ww0", "ww1", "k0", "k1", "r0", "r1"])
FRONT_INDEX = {name: k for k, name in enumerate(FRONT_USES)}
FRONT_BANKS = 3
FRONT_TURNS = len(FRONT_USES) // FRONT_BANKS
assert len(FRONT_USES) % FRONT_BANKS == 0
SLOT = {"tok0": 1, "tok1": 2, "mean": 5, "var": 8, "g0": 9, "g1": 10, "m": 12, "m4": 13, "delta": 15, "td": 20,
        "v0": 21, "v1": 22, "ww": 23, "k0": 24, "k1": 25, "r0": 26, "r1": 27,
        "ruk0": 1, "ruk1": 3, "cent0": 28, "var0": 30,
        "cent1": 7, "var1": 8, "rows0": 14, "rows1": 16}
HEAD_USES = ["cent0", "var0"]
TAIL_USES = ["cent1", "var1", "rows0", "rows1"]
HU, TU = len(HEAD_USES), len(TAIL_USES)


def splits(u):
    return sum(n not in WHOLE for n in range(u))


def bank_turns(use, w, before=False):
    k = FRONT_INDEX[use]
    gate = ("g0", "g1")
    first, last = isinstance(w, int) and w == 0, isinstance(w, int) and w == NG
    here = [name for n, name in enumerate(FRONT_USES) if n % FRONT_BANKS == k % FRONT_BANKS]
    this_walk = [name for name in here if FRONT_INDEX[name] < k + (0 if before else 1)]
    if first:
        return sum(name not in gate for name in this_walk)
    if last:
        this_walk = [name for name in this_walk if name in gate]
    return w * FRONT_TURNS + (len(this_walk) - sum(name in gate for name in here))


def wait(eng, sem, value):
    if isinstance(value, int) and value <= 0:
        return
    eng.wait_ge(sem, value)


def walk(eng, slot):
    def one(scan, front, tail):
        for u in range(UNITS):
            slot(u, scan, front, tail)

    def at(g):
        return (g, g % 2, g // 2) if 0 <= g < NG else None

    one(None, at(0), None)
    one(at(0), at(1), None)
    one(at(1), at(2), at(0))
    with eng.Fori(1, NG // 2 - 1) as i:
        one((i * 2, 0, i), (i * 2 + 1, 1, i), (i * 2 - 1, 1, i - 1))
        one((i * 2 + 1, 1, i), (i * 2 + 2, 0, i + 1), (i * 2, 0, i))
    for g in range(NG - 2, NG + 1):
        one(at(g), at(g + 1), at(g - 1))


def attention_phase(nc, d, const):
    ident, params, ready = const
    with ExitStack() as ctx:
        def sb(name, shape, dt=F32):
            return ctx.enter_context(nc.sbuf_tensor(name, shape, dt))

        def ps(name, shape):
            return ctx.enter_context(nc.psum_tensor(name, shape, F32))

        def sem(name):
            return ctx.enter_context(nc.semaphore(name))

        w_tok = sb("w_tok", [P, NC, C])
        w_r = sb("w_r", [P, NC, C])
        w_k = sb("w_k", [P, NC, C])
        w_v = sb("w_v", [P, NC, C])
        w_g = sb("w_g", [P, NC, C])
        w_o = sb("w_o", [P, NC, C])
        tm_w1 = sb("tm_w1", [P, NC, NMIX * LORA])
        tm_w2 = sb("tm_w2", [P, C])
        tm_w2_last = sb("tm_w2_last", [LORA, C])
        td_w1 = sb("td_w1", [P, NC, DW])
        td_w2 = sb("td_w2", [DW, C])
        head_u = sb("head_u", [P, NC, P])
        head_mean = sb("head_mean", [P, P])
        head_cent = sb("head_cent", [P, P])
        value_sum = sb("value_sum", [P, K, P], F32R)
        value_sel = sb("value_sel", [P, K, P], F32R)
        mean_w = sb("mean_w", [P, P])
        eps4 = sb("eps4", [P, 1])
        eps1 = sb("eps1", [P, 1])
        half_ln = sb("half_ln", [P, 2 * NC])

        x_in = sb("x_in", [P, 2 * NC, GT])
        diff = sb("diff", [P, NC, GT])
        summ = sb("summ", [P, NC, GT])
        th = sb("th", [P, NC, GT])
        y_sq0 = sb("y_sq0", [P, GT])
        y_sq = [y_sq0[:], th[:, 1, :]]
        h2 = sb("h2", [P, NC, GT])
        h_res = sb("h_res", [P, 2, NC, GT])
        cent = sb("cent", [P, NC, GT])
        sq_xxx = sb("sq_xxx", [P, NC, GT])
        rstd = sb("rstd", [P, GT])
        xn = sb("xn", [P, NC, GB, T + 1])
        sx = sb("sx", [P, NC, GT])
        m_a = sb("m_a", [P, GT])
        m_b = sb("m_b", [LORA, GT])
        x_f = sb("x_f", [P, NMIX, NC, GT])
        x_f_flat = x_f[:].rearrange("p f c n -> p (f c n)")
        td_h = sb("td_h", [DW, GT])
        w_s = sb("w_s", [P, 2, NC, GB, T])
        k_s = sb("k_s", [P, 2, NC, GT])
        r_s = sb("r_s", [P, 2, NC, GB, T])
        v_f = x_f[:, 0]
        rk = x_f[:, 1]
        v_p = [sb(f"v_p{n}", [P, 2, NC, GT], F32R) for n in range(2)]
        gate = sb("gate", [P, 2, NC, GT])
        y_now = sb("y_now", [P, 2, NC, GT])
        kv = sb("kv", [P, 2, GT])
        state = sb("state", [P, RING, GT + 1])
        rs = sb("rs", [P, RING, GT])
        rs_hi = sb("rs_hi", [P, RING, GT], F32R)
        rs_lo = sb("rs_lo", [P, 2, GT], F32R)
        y = sb("y", [P, NC, GT])
        rows = sb("rows", [P, GB, C])

        bank = [ps(f"front{n}", [P, 512]) for n in range(FRONT_BANKS)]
        tail_bank = ps("tail_bank", [P, 512])
        vrep = [ps(f"vrep{n}", [P, 512]) for n in range(2)]
        y_ps = [ps(f"y_ps{n}", [P, 512]) for n in range(NC)]

        w_ready = ready
        made = sem("made")
        front_filled = [sem(f"front_filled{n}") for n in range(FRONT_BANKS)]
        front_read = [sem(f"front_read{n}") for n in range(FRONT_BANKS)]
        head_filled = sem("head_filled")
        head_read = sem("head_read")
        tail_filled = sem("tail_filled")
        tail_read = sem("tail_read")
        x_loaded = sem("x_loaded")
        diff_ready = sem("diff_ready")
        summ_ready = sem("summ_ready")
        gated = sem("gated")
        h_ready = sem("h_ready")
        res_ready = sem("res_ready")
        squared = sem("squared")
        rstd_ready = sem("rstd_ready")
        xn_ready = sem("xn_ready")
        sx_ready = sem("sx_ready")
        xxx_ready = sem("xxx_ready")
        xf_ready = sem("xf_ready")
        decay_ready = sem("decay_ready")
        r_ready = sem("r_ready")
        tg_ready = sem("tg_ready")
        v_part = [sem(f"v_part{n}") for n in range(2)]
        vrep_ready = sem("vrep_ready")
        kv_ready = sem("kv_ready")
        scanned = sem("scanned")
        rs_ready = sem("rs_ready")
        hi_ready = sem("hi_ready")
        lo_ready = sem("lo_ready")
        y_part = sem("y_part")
        y_read = sem("y_read")
        ruk_filled = sem("ruk_filled")
        ruk_read = sem("ruk_read")
        y_squared = sem("y_squared")
        yrstd_ready = sem("yrstd_ready")
        yn_ready = sem("yn_ready")
        affine_ready = sem("affine_ready")
        z_ready = sem("z_ready")
        stored = sem("stored")

        x_dram = d["x"].rearrange("a (c p) n -> p (a c) n", p=P)
        out_dram = d["out"].rearrange("b t c -> t b c")

        def filled(eng, use, g):
            wait(eng, fill_sem(use), bank_turns(use, g))

        def was_read(eng, use, g):
            wait(eng, read_sem(use), bank_turns(use, g))

        def free(eng, use, g):
            wait(eng, read_sem(use), bank_turns(use, g, before=True))

        def bank_of(use):
            return bank[FRONT_INDEX[use] % FRONT_BANKS]

        def fill_sem(use):
            return front_filled[FRONT_INDEX[use] % FRONT_BANKS]

        def read_sem(use):
            return front_read[FRONT_INDEX[use] % FRONT_BANKS]

        def by_seq(ap):
            return ap.rearrange("p (b t) -> p b t", b=GB)

        block = ctx.enter_context(nc.Block())

        @block.sync
        def _(sp):
            weights = [(w_tok, "tok_w"), (w_r, "Wr"), (w_k, "Wk"), (w_v, "Wv"), (w_g, "Wg"), (w_o, "Wo"),
                       (tm_w1, "tm_w1"), (td_w1, "td_w1")]

            def load(g):
                sp.dma_start(x_in[:], x_dram[:, :, bass.ds(g * GT, GT)]).then_inc(x_loaded, 16)

            load(0)
            for tile, name in weights:
                sp.dma_start(tile[:], d[name].rearrange("(c p) n -> p c n", p=P)).then_inc(w_ready, 16)
            sp.dma_start(tm_w2[:], d["tm_w2"][0:P, :]).then_inc(w_ready, 16)
            sp.dma_start(tm_w2_last[:], d["tm_w2"][P:P + LORA, :]).then_inc(w_ready, 16)
            sp.dma_start(td_w2[:], d["td_w2"]).then_inc(w_ready, 16)
            sp.dma_start(head_mean[:], d["head_block"]).then_inc(w_ready, 16)
            sp.dma_start(x_f_flat[:, 0:K * P], d["value_sel"]).then_inc(w_ready, 16)
            sp.dma_start(x_f_flat[:, K * P:2 * K * P], d["value_sum"]).then_inc(w_ready, 16)

            def slot(u, scan, front, tail):
                if u == 3 and front is not None:
                    g, par, half = front
                    if not (isinstance(g, int) and g + 1 >= NG):
                        wait(sp, diff_ready, g + 1)
                        wait(sp, summ_ready, g + 1)
                        load(g + 1)
                if u == SLOT["rows1"] + 1 and tail is not None:
                    g, par, half = tail
                    wait(sp, tail_read, g * TU + TU)
                    sp.dma_start(out_dram[:, bass.ds(g * GB, GB), :], rows[0:T]).then_inc(stored, 16)

            walk(sp, slot)
            sp.wait_ge(stored, 16 * NG)

        @block.tensor
        def _(pe):
            pe.wait_ge(w_ready, 16 * 17)
            pe.wait_ge(made, 14)

            def dense(use, g, weights, moving, m=P, cols=None):
                free(pe, use, g)
                for c in range(NC):
                    last = nc.tensor.matmul(bank_of(use)[0:m, 0:GT], weights(c), moving(c),
                                            start=(c == 0), stop=(c == NC - 1))
                last.then_inc(fill_sem(use), 1)

            def ysum(u, g):
                c, v = divmod(u, K)
                if u in WHOLE:
                    wait(pe, rs_ready, g * UNITS + u + 1)
                else:
                    wait(pe, lo_ready, g * SPLITS + splits(u) + 1)
                if v == 0:
                    wait(pe, y_read, g * NC + c - 1)
                weights = value_sum[:, v, :]
                parts = [(weights, rs_hi[:, u % RING, :]), (weights, rs_lo[:, u % 2, :])]
                if u in WHOLE:
                    parts = [(weights.bitcast(F32), rs[:, u % RING, :])]
                for n, (w, part) in enumerate(parts):
                    last = nc.tensor.matmul(y_ps[c][:, 0:GT], w, part, start=(v == 0 and n == 0),
                                            stop=(v == K - 1 and n == len(parts) - 1))
                last.then_inc(y_part, 1)

            def slot(u, scan, front, tail):
                if scan is not None:
                    g, par, half = scan
                    c, v = divmod(u, K)
                    if u == 0:
                        wait(pe, v_part[1], g + 1)
                    wait(pe, kv_ready, g * UNITS + u - 1)
                    for n in range(2):
                        last = nc.tensor.matmul(vrep[u % 2][:, 0:GT], value_sel[:, v, :], v_p[n][:, par, c, :],
                                                start=(n == 0), stop=(n == 1))
                    last.then_inc(vrep_ready, 1)
                    if u >= YLAG:
                        ysum(u - YLAG, g)
                if u < YLAG and tail is not None:
                    ysum(UNITS - YLAG + u, tail[0])
                if front is not None:
                    g, par, half = front
                    for c in range(NC):
                        if u == SLOT[f"tok{c}"]:
                            if c == 0:
                                wait(pe, diff_ready, g + 1)
                            dense(f"tok{c}", g, lambda i: w_tok[:, i, c * P:(c + 1) * P], lambda i: diff[:, i, :])
                    if u == SLOT["mean"]:
                        wait(pe, h_ready, g + 1)
                        dense("mean", g, lambda c: mean_w[:], lambda c: h2[:, c, :])
                    if u == SLOT["var"]:
                        wait(pe, squared, g + 1)
                        dense("var", g, lambda c: mean_w[:], lambda c: sq_xxx[:, c, :])
                    if u == SLOT["m"]:
                        wait(pe, xxx_ready, g * NC + NC)
                        dense("m", g, lambda c: tm_w1[:, c, 0:P], lambda c: sq_xxx[:, c, :])
                    if u == SLOT["m4"]:
                        dense("m4", g, lambda c: tm_w1[:, c, P:P + LORA], lambda c: sq_xxx[:, c, :], m=LORA)
                    if SLOT["delta"] <= u < SLOT["delta"] + NMIX:
                        f = u - SLOT["delta"]
                        if f == 0:
                            was_read(pe, "m", g)
                        if f == NMIX - 1:
                            was_read(pe, "m4", g)
                        for c in range(NC):
                            use = f"delta{f}{c}"
                            free(pe, use, g)
                            cols = slice(c * P, (c + 1) * P)
                            if f < NMIX - 1:
                                part = slice(f * LORA, (f + 1) * LORA)
                                w2, m = tm_w2[part, cols], m_a[part, :]
                            else:
                                w2, m = tm_w2_last[:, cols], m_b[:]
                            nc.tensor.matmul(bank_of(use)[:, 0:GT], w2, m, start=True, stop=True) \
                                .then_inc(fill_sem(use), 1)
                    if u == SLOT["td"]:
                        wait(pe, xf_ready, g * NMIX + 1)
                        dense("td", g, lambda c: td_w1[:, c, :], lambda c: x_f[:, 0, c, :], m=DW)
                    if u == SLOT["ww"]:
                        was_read(pe, "td", g)
                        for c in range(NC):
                            use = f"ww{c}"
                            free(pe, use, g)
                            nc.tensor.matmul(bank_of(use)[:, 0:GT], td_w2[:, c * P:(c + 1) * P], td_h[:],
                                             start=True, stop=True).then_inc(fill_sem(use), 1)
                    for f, (name, weight) in enumerate((("k", w_k), ("v", w_v), ("r", w_r)), 1):
                        for c in range(NC):
                            if u == SLOT[f"{name}{c}"]:
                                wait(pe, xf_ready, g * NMIX + f + 1)
                                dense(f"{name}{c}", g, lambda i: weight[:, i, c * P:(c + 1) * P],
                                      lambda i: x_f[:, f, i, :])
                if scan is not None:
                    g, par, half = scan
                    for c in range(NC):
                        if u == SLOT[f"g{c}"]:
                            dense(f"g{c}", g + 1, lambda i: w_g[:, i, c * P:(c + 1) * P],
                                  lambda i: x_f[:, NMIX - 1, i, :])
                    for c in range(NC):
                        if u == SLOT[f"ruk{c}"]:
                            was_read(pe, f"r{c}", g)
                            if c == 0:
                                wait(pe, head_read, g * HU)
                            else:
                                wait(pe, ruk_read, g * NC + 1)
                            nc.tensor.matmul(tail_bank[:, 0:GT], head_u[:, c, :], rk[:, c, :], start=True,
                                             stop=True).then_inc(ruk_filled, 1)
                    if u == SLOT["cent0"]:
                        wait(pe, ruk_read, g * NC + NC)
                        wait(pe, tail_read, g * TU)
                        wait(pe, y_read, g * NC + 1)
                        nc.tensor.matmul(tail_bank[:, 0:GT], head_cent[:], y[:, 0, :], start=True, stop=True) \
                            .then_inc(head_filled, 1)
                    if u == SLOT["var0"]:
                        wait(pe, head_read, g * HU + 1)
                        wait(pe, y_squared, g * NC + 1)
                        nc.tensor.matmul(tail_bank[:, 0:GT], head_mean[:], y_sq[0], start=True, stop=True) \
                            .then_inc(head_filled, 1)
                if tail is not None:
                    g, par, half = tail
                    if u == SLOT["cent1"]:
                        last_ruk = (g + 1) * NC + NC
                        wait(pe, ruk_read, min(last_ruk, NG * NC) if isinstance(g, int) else last_ruk)
                        wait(pe, head_read, g * HU + HU)
                        wait(pe, y_read, g * NC + NC)
                        nc.tensor.matmul(tail_bank[:, 0:GT], head_cent[:], y[:, 1, :], start=True, stop=True) \
                            .then_inc(tail_filled, 1)
                    if u == SLOT["var1"]:
                        wait(pe, tail_read, g * TU + 1)
                        wait(pe, y_squared, g * NC + NC)
                        nc.tensor.matmul(tail_bank[:, 0:GT], head_mean[:], y_sq[1], start=True, stop=True) \
                            .then_inc(tail_filled, 1)
                    for j in range(2):
                        if u == SLOT[f"rows{j}"]:
                            if j == 0:
                                wait(pe, z_ready, g * NC + NC)
                                wait(pe, res_ready, g + 1)
                            wait(pe, tail_read, g * TU + 2 + j)
                            for b in range(2):
                                seq = slice((2 * j + b) * T, (2 * j + b + 1) * T)
                                for c in range(NC):
                                    nc.tensor.matmul(tail_bank[0:T, b * C:(b + 1) * C], y[:, c, seq], w_o[:, c, :],
                                                     start=(c == 0), stop=False, skip_group_check=True)
                                for c in range(NC):
                                    at = b * C + c * P
                                    last = nc.tensor.matmul(tail_bank[0:T, at:at + P], h_res[:, par, c, seq],
                                                            ident[:], start=False, stop=(c == NC - 1),
                                                            skip_group_check=True)
                            last.then_inc(tail_filled, 1)

            walk(pe, slot)

        @block.vector
        def _(dve):
            nc.vector.memset(mean_w[:], 1.0 / C).then_inc(made, 1)
            nc.vector.memset(eps4[:], 4 * EPS).then_inc(made, 1)
            nc.vector.memset(eps1[:], EPS).then_inc(made, 1)
            nc.vector.memset(w_s[:], 0.0).then_inc(made, 1)
            nc.vector.memset(r_s[:], 0.0).then_inc(made, 1)
            nc.vector.memset(state[:], 0.0).then_inc(made, 1)
            nc.vector.memset(xn[:], 0.0).then_inc(made, 1)
            dve.wait_ge(w_ready, 16 * 17)
            nc.vector.tensor_copy(value_sel[:], x_f_flat[:, 0:K * P].rearrange("p (v q) -> p v q", v=K)) \
                .then_inc(made, 1)
            nc.vector.tensor_copy(value_sum[:], x_f_flat[:, K * P:2 * K * P].rearrange("p (v q) -> p v q", v=K)) \
                .then_inc(made, 1)
            for c in range(NC):
                u_col = params[:, COL["u"] + c:COL["u"] + c + 1]
                nc.vector.tensor_scalar(head_u[:, c, :], head_mean[:], u_col, None, ALU.mult).then_inc(made, 1)
            dve.wait_ge(made, 11)
            nc.vector.tensor_scalar(head_mean[:], head_mean[:], 1.0 / K, None, ALU.mult).then_inc(made, 1)
            dve.wait_ge(made, 12)
            nc.vector.tensor_tensor(head_cent[:], ident[:], head_mean[:], ALU.subtract).then_inc(made, 1)
            nc.vector.tensor_scalar(half_ln[:], params[:, COL["ln_w"]:COL["ln_w"] + 2 * NC], 0.5, None,
                                    ALU.mult).then_inc(made, 1)
            dve.wait_ge(made, 14)

            def scan_unit(u, g, par):
                c = u // K
                if u == 0:
                    wait(dve, decay_ready, g * NC + NC)
                wait(dve, kv_ready, g * UNITS + u + 1)
                wait(dve, rs_ready, g * UNITS + u + 1 - RING)
                nc.vector.tensor_tensor_scan(state[:, u % RING, 1:GT + 1],
                                             w_s[:, par, c].rearrange("p b t -> p (b t)"), kv[:, u % 2, :],
                                             0.0, ALU.mult, ALU.add).then_inc(scanned, 1)

            def lo_unit(u, g):
                if u in WHOLE:
                    return
                wait(dve, hi_ready, g * SPLITS + splits(u) + 1)
                wait(dve, y_part, g * UNITS + u - 1)
                nc.vector.tensor_tensor(rs_lo[:, u % 2, :], rs[:, u % RING, :],
                                        rs_hi[:, u % RING, :].bitcast(F32), ALU.subtract).then_inc(lo_ready, 1)

            def take_y(c, group):
                g, par, half = group
                wait(dve, y_part, g * UNITS + (c + 1) * K)
                wait(dve, ruk_read, g * NC + c + 1)
                wait(dve, tail_filled, g * TU)
                nc.vector.tensor_tensor(y[:, c, :], y_ps[c][:, 0:GT], y_now[:, par, c, :], ALU.add) \
                    .then_inc(y_read, 1)

            def slot(u, scan, front, tail):
                if scan is not None and u >= LO_LAG:
                    lo_unit(u - LO_LAG, scan[0])
                if u < LO_LAG and tail is not None:
                    lo_unit(UNITS - LO_LAG + u, tail[0])
                if scan is not None:
                    g, par, half = scan
                    c = u // K
                    if u == 0:
                        was_read(dve, "k0", g)
                        was_read(dve, "k1", g)
                    wait(dve, vrep_ready, g * UNITS + u + 1)
                    wait(dve, scanned, g * UNITS + u - 1)
                    nc.vector.tensor_tensor(kv[:, u % 2, :], vrep[u % 2][:, 0:GT], k_s[:, par, c, :],
                                            ALU.mult).then_inc(kv_ready, 1)
                    if u >= 1:
                        scan_unit(u - 1, g, par)
                if u == 0 and tail is not None:
                    scan_unit(UNITS - 1, tail[0], tail[1])
                if u == K + YLAG and scan is not None:
                    take_y(0, scan)
                if u == YLAG and tail is not None:
                    take_y(1, tail)
                if front is not None:
                    g, par, half = front
                    if u == 3:
                        was_read(dve, "tok0", g)
                        was_read(dve, "tok1", g)
                        nc.vector.tensor_tensor(th[:], th[:], diff[:], ALU.mult).then_inc(gated, 1)
                    if u == 4:
                        wait(dve, gated, g + 1)
                        wait(dve, summ_ready, g + 1)
                        wait(dve, res_ready, g)
                        nc.vector.tensor_tensor(h2[:], th[:], summ[:], ALU.add).then_inc(h_ready, 1)
                    if u == 6:
                        filled(dve, "mean", g)
                        mean = bank_of("mean")[:, 0:GT].unsqueeze(1).to_broadcast([P, NC, GT])
                        nc.vector.tensor_tensor(cent[:], h2[:], mean, ALU.subtract).then_inc(read_sem("mean"), 1)
                    if u == 9:
                        wait(dve, rstd_ready, g + 1)
                        wait(dve, xf_ready, g * NMIX)
                        for c in range(NC):
                            last = nc.vector.tensor_tensor(xn[:, c, :, 1:T + 1], by_seq(cent[:, c, :]),
                                                           by_seq(rstd[:]), ALU.mult)
                        last.then_inc(xn_ready, 1)
                    if u == 11:
                        wait(dve, sx_ready, g + 1)
                        for c in range(NC):
                            maa_x = params[:, COL["maa_x"] + c:COL["maa_x"] + c + 1]
                            nc.vector.scalar_tensor_tensor(by_seq(sq_xxx[:, c, :]), by_seq(sx[:, c, :]), maa_x,
                                                           xn[:, c, :, 1:T + 1], ALU.mult, ALU.add) \
                                .then_inc(xxx_ready, 1)
                    if SLOT["delta"] <= u < SLOT["delta"] + NMIX:
                        f = u - SLOT["delta"]
                        for c in range(NC):
                            use = f"delta{f}{c}"
                            maa = params[:, COL["maa"] + f * NC + c:COL["maa"] + f * NC + c + 1]
                            filled(dve, use, g)
                            if f == 0 and c == 0:
                                wait(dve, v_part[1], g)
                                wait(dve, ruk_read, g * NC)
                            nc.vector.scalar_tensor_tensor(x_f[:, f, c, :], bank_of(use)[:, 0:GT], maa,
                                                           sx[:, c, :], ALU.add, ALU.mult) \
                                .then_inc(read_sem(use), 1)
                    for c in range(NC):
                        use = f"r{c}"
                        if u == SLOT[use] + 1:
                            was_read(dve, "k1", g)
                            wait(dve, r_ready, g * NC + c + 1)
                            nc.vector.tensor_tensor(rk[:, c, :], bank_of(use)[:, 0:GT], k_s[:, par, c, :],
                                                    ALU.mult).then_inc(read_sem(use), 1)
                if scan is not None:
                    g, par, half = scan
                    for c in range(NC):
                        if u == SLOT[f"ruk{c}"] + 1:
                            wait(dve, ruk_filled, g * NC + c + 1)
                            nc.vector.tensor_tensor(y_now[:, par, c, :], tail_bank[:, 0:GT], v_f[:, c, :],
                                                    ALU.mult).then_inc(ruk_read, 1)
                    for c in range(NC):
                        use = f"g{c}"
                        if u == SLOT[use] + 1:
                            wait(dve, tg_ready, g * NC + c + 1)
                            nc.vector.scalar_tensor_tensor(gate[:, par, c, :], gate[:, par, c, :], 1.0,
                                                           bank_of(use)[:, 0:GT], ALU.add, ALU.mult) \
                                .then_inc(read_sem(use), 1)
                    if u == SLOT["var0"] + 1:
                        wait(dve, yrstd_ready, g * NC + 1)
                        nc.vector.tensor_tensor(y[:, 0, :], y[:, 0, :], y_sq[0], ALU.mult).then_inc(yn_ready, 1)
                if tail is not None:
                    g, par, half = tail
                    if u == SLOT["var1"] + 2:
                        wait(dve, yrstd_ready, g * NC + NC)
                        nc.vector.tensor_tensor(y[:, 1, :], y[:, 1, :], y_sq[1], ALU.mult).then_inc(yn_ready, 1)

            walk(dve, slot)

        @block.gpsimd
        def _(pool):
            pool.wait_ge(made, 14)

            def rs_unit(u, g, par):
                wait(pool, scanned, g * UNITS + u + 1)
                if u == 0:
                    wait(pool, r_ready, g * NC + NC)
                held, its_g = (u - RING, g) if u >= RING else (u - RING + UNITS, g - 1)
                if held in WHOLE:
                    wait(pool, y_part, its_g * UNITS + held + 1)
                else:
                    wait(pool, lo_ready, its_g * SPLITS + splits(held) + 1)
                nc.gpsimd.tensor_tensor(rs[:, u % RING, :], r_s[:, par, u // K].rearrange("p b t -> p (b t)"),
                                        state[:, u % RING, 0:GT], ALU.mult).then_inc(rs_ready, 1)

            def slot(u, scan, front, tail):
                if u == 0 and front is not None:
                    g = front[0]
                    wait(pool, x_loaded, g * 16 + 16)
                    wait(pool, h_ready, g)
                    nc.gpsimd.tensor_tensor(diff[:], x_in[:, 0:NC], x_in[:, NC:2 * NC],
                                            ALU.subtract).then_inc(diff_ready, 1)
                if scan is not None and u >= 2:
                    rs_unit(u - 2, scan[0], scan[1])
                if u < 2 and tail is not None:
                    rs_unit(UNITS - 2 + u, tail[0], tail[1])
                if front is not None:
                    g, par, half = front
                    if u == 2:
                        nc.gpsimd.tensor_tensor(summ[:], x_in[:, 0:NC], x_in[:, NC:2 * NC],
                                                ALU.add).then_inc(summ_ready, 1)
                    if u == 10:
                        wait(pool, xn_ready, g + 1)
                        for c in range(NC):
                            last = nc.gpsimd.tensor_tensor(by_seq(sx[:, c, :]), xn[:, c, :, 0:T],
                                                           xn[:, c, :, 1:T + 1], ALU.subtract)
                        last.then_inc(sx_ready, 1)
                    if SLOT["delta"] < u <= SLOT["delta"] + NMIX:
                        f = u - SLOT["delta"] - 1
                        was_read(pool, f"delta{f}0", g)
                        was_read(pool, f"delta{f}1", g)
                        for c in range(NC):
                            last = nc.gpsimd.tensor_tensor(by_seq(x_f[:, f, c, :]), by_seq(x_f[:, f, c, :]),
                                                           xn[:, c, :, 1:T + 1], ALU.add)
                        last.then_inc(xf_ready, 1)
                    if u == SLOT["v1"] + 1:
                        wait(pool, v_part[0], g + 1)
                        nc.gpsimd.tensor_tensor(v_p[1][:, par], v_f[:], v_p[0][:, par].bitcast(F32), ALU.subtract) \
                            .then_inc(v_part[1], 1)
                if tail is not None:
                    g, par, half = tail
                    for c in range(NC):
                        if u == (3, SLOT["var1"] + 3)[c]:
                            wait(pool, affine_ready, g * NC + c + 1)
                            nc.gpsimd.tensor_tensor(y[:, c, :], y[:, c, :], gate[:, par, c, :], ALU.mult) \
                                .then_inc(z_ready, 1)

            walk(pool, slot)

        @block.scalar
        def _(act):
            act.wait_ge(w_ready, 16 * 17)
            act.wait_ge(made, 14)

            def column(name, c):
                return params[:, COL[name] + c:COL[name] + c + 1]

            def hi_unit(u, g):
                if u in WHOLE:
                    return
                wait(act, y_part, g * UNITS + u + 1 - RING)
                wait(act, rs_ready, g * UNITS + u + 1)
                nc.scalar.copy(rs_hi[:, u % RING, :], rs[:, u % RING, :]).then_inc(hi_ready, 1)

            def slot(u, scan, front, tail):
                if scan is not None and u >= HI_LAG:
                    hi_unit(u - HI_LAG, scan[0])
                if u < HI_LAG and tail is not None:
                    hi_unit(UNITS - HI_LAG + u, tail[0])
                if front is not None:
                    g, par, half = front
                    for c in range(NC):
                        use = f"tok{c}"
                        if u == SLOT[use]:
                            wait(act, h_ready, g)
                            filled(act, use, g)
                            nc.scalar.activation(th[:, c, :], bank_of(use)[:, 0:GT], ACT.Tanh, scale=0.5) \
                                .then_inc(read_sem(use), 1)
                    if u == 6:
                        was_read(act, "mean", g)
                        nc.scalar.activation(sq_xxx[:], cent[:], ACT.Square).then_inc(squared, 1)
                    if u == SLOT["m4"]:
                        filled(act, "m", g)
                        nc.scalar.activation(m_a[:], bank_of("m")[:, 0:GT], ACT.Tanh).then_inc(read_sem("m"), 1)
                        filled(act, "m4", g)
                        nc.scalar.activation(m_b[:], bank_of("m4")[0:LORA, 0:GT], ACT.Tanh) \
                            .then_inc(read_sem("m4"), 1)
                    if u == SLOT["td"]:
                        filled(act, "td", g)
                        nc.scalar.activation(td_h[:], bank_of("td")[0:DW, 0:GT], ACT.Tanh) \
                            .then_inc(read_sem("td"), 1)
                    if u == SLOT["ww"]:
                        wait(act, scanned, g * UNITS - UNITS)
                        for c in range(NC):
                            use = f"ww{c}"
                            filled(act, use, g)
                            nc.scalar.activation(w_s[:, par, c, :, 1:T], by_seq(bank_of(use)[:, 0:GT])[:, :, 1:T],
                                                 ACT.Exp, bias=column("decay", c)).then_inc(read_sem(use), 1)
                        for c in range(NC):
                            was_read(act, f"ww{c}", g)
                            nc.scalar.activation(w_s[:, par, c, :, 1:T], w_s[:, par, c, :, 1:T], ACT.Exp,
                                                 scale=-1.0).then_inc(decay_ready, 1)
                    for c in range(NC):
                        use = f"k{c}"
                        if u == SLOT[use]:
                            wait(act, kv_ready, g * UNITS - UNITS)
                            filled(act, use, g)
                            nc.scalar.copy(k_s[:, par, c, :], bank_of(use)[:, 0:GT]).then_inc(read_sem(use), 1)
                    if u == SLOT["v1"]:
                        wait(act, v_part[1], g)
                        wait(act, ruk_read, g * NC)
                        for c in range(NC):
                            use = f"v{c}"
                            filled(act, use, g)
                            nc.scalar.copy(v_f[:, c, :], bank_of(use)[:, 0:GT]).then_inc(read_sem(use), 1)
                        was_read(act, "v0", g)
                        was_read(act, "v1", g)
                        wait(act, vrep_ready, g * UNITS - UNITS)
                        nc.scalar.copy(v_p[0][:, par], v_f[:]).then_inc(v_part[0], 1)
                    for c in range(NC):
                        use = f"r{c}"
                        if u == SLOT[use]:
                            wait(act, rs_ready, g * UNITS - UNITS)
                            filled(act, use, g)
                            nc.scalar.copy(r_s[:, par, c, :, 1:T], by_seq(bank_of(use)[:, 0:GT])[:, :, 1:T]) \
                                .then_inc(r_ready, 1)
                    if u == 18:
                        wait(act, tail_filled, g * TU - TU)
                        nc.scalar.mul(h_res[:, par], h2[:], 0.5).then_inc(res_ready, 1)
                if scan is not None:
                    g, par, half = scan
                    for c in range(NC):
                        use = f"g{c}"
                        if u == SLOT[use]:
                            wait(act, z_ready, (g - 1) * NC)
                            filled(act, use, g + 1)
                            nc.scalar.activation(gate[:, par, c, :], bank_of(use)[:, 0:GT], ACT.Tanh, scale=0.5) \
                                .then_inc(tg_ready, 1)
                    if u == SLOT["cent0"]:
                        wait(act, yn_ready, g * NC - 1)
                        wait(act, head_filled, g * HU + 1)
                        nc.scalar.activation(y_sq[0], tail_bank[:, 0:GT], ACT.Square).then_inc(y_squared, 1)
                        nc.scalar.copy(y[:, 0, :], tail_bank[:, 0:GT]).then_inc(head_read, 1)
                    if u == SLOT["var0"]:
                        wait(act, head_filled, g * HU + 2)
                        nc.scalar.activation(y_sq[0], tail_bank[:, 0:GT], ACT.Ln, bias=eps1[:]).then_inc(head_read, 1)
                        wait(act, head_read, g * HU + 2)
                        nc.scalar.activation(y_sq[0], y_sq[0], ACT.Exp, scale=-0.5).then_inc(yrstd_ready, 1)
                if u == SLOT["var"] and front is not None:
                    g = front[0]
                    filled(act, "var", g)
                    wait(act, xn_ready, g)
                    nc.scalar.activation(rstd[:], bank_of("var")[:, 0:GT], ACT.Ln, bias=eps4[:]) \
                        .then_inc(read_sem("var"), 1)
                if u == SLOT["var1"] and tail is not None:
                    g = tail[0]
                    wait(act, tail_filled, g * TU + 2)
                    nc.scalar.activation(y_sq[1], tail_bank[:, 0:GT], ACT.Ln, bias=eps1[:]).then_inc(tail_read, 1)
                if u == SLOT["var"] and front is not None:
                    was_read(act, "var", front[0])
                    nc.scalar.activation(rstd[:], rstd[:], ACT.Exp, scale=-0.5).then_inc(rstd_ready, 1)
                if u == SLOT["var1"] and tail is not None:
                    wait(act, tail_read, tail[0] * TU + 2)
                    nc.scalar.activation(y_sq[1], y_sq[1], ACT.Exp, scale=-0.5).then_inc(yrstd_ready, 1)
                if tail is not None:
                    g, par, half = tail
                    for c in range(NC):
                        if u == (0, SLOT["var1"] + 2)[c]:
                            wait(act, yn_ready, g * NC + c + 1)
                            nc.scalar.activation(y[:, c, :], y[:, c, :], ACT.Identity,
                                                 bias=half_ln[:, NC + c:NC + c + 1],
                                                 scale=half_ln[:, c:c + 1]).then_inc(affine_ready, 1)
                    if u == SLOT["cent1"]:
                        wait(act, h_ready, min(g + 3, NG) if isinstance(g, int) else g + 3)
                        wait(act, tail_filled, g * TU + 1)
                        nc.scalar.activation(y_sq[1], tail_bank[:, 0:GT], ACT.Square).then_inc(y_squared, 1)
                        nc.scalar.copy(y[:, 1, :], tail_bank[:, 0:GT]).then_inc(tail_read, 1)
                    for j in range(2):
                        if u == SLOT[f"rows{j}"]:
                            wait(act, tail_filled, g * TU + 3 + j)
                            if j == 0:
                                wait(act, stored, g * 16)
                            nc.scalar.copy(rows[0:T, 2 * j:2 * j + 2, :],
                                           tail_bank[0:T, :].rearrange("p (b c) -> p b c", b=2)) \
                                .then_inc(tail_read, 1)

            walk(act, slot)


def expert_phase(nc, d, const, idx):
    ident, params, ready = const
    with ExitStack() as ctx:
        def sb(name, shape, dt=F32):
            return ctx.enter_context(nc.sbuf_tensor(name, shape, dt))

        def ps(name, shape):
            return ctx.enter_context(nc.psum_tensor(name, shape, F32))

        def sem(name):
            return ctx.enter_context(nc.semaphore(name))

        idx_f = sb("idx_f", [P, NT])
        spare = sb("spare", [P, 1])
        earlier = sb("earlier", [P, P])
        ones_row = sb("ones_row", [1, P])
        b1 = sb("b1", [P, E, NF])
        b2 = sb("b2", [1, E, C])
        w1 = sb("w1", [P, 2, NC, FF])
        w2 = sb("w2", [P, 2, NF, C])
        got = sb("got", [P, NT, C])
        got_w = sb("got_w", [P, NT, E])
        stats = sb("stats", [P, NT, 6])
        moments = sb("moments", [P, NT, 2])
        rstd = sb("rstd2", [P, NT])
        neg_half = sb("neg_half", [P, 1])
        normed = sb("normed", [P, TPE, C])
        xT = sb("xT", [P, 2, NC, CAP])
        hid = sb("hid", [P, NF, CAP])
        weighted = sb("weighted", [P, 2, C])
        same = sb("same", [P, 2, P])
        same_before = sb("same_before", [P, P])
        dups = sb("dups", [P, NT])
        shift_f = sb("shift_f", [P, NT])
        target = sb("target", [P, NT], I32)
        summed = sb("summed", [P, 2, C])
        zero = sb("zero", [P, C])

        t_ps = [ps(f"t_ps{n}", [P, 512]) for n in range(2)]
        h_ps = [ps(f"h_ps{n}", [P, 512]) for n in range(2)]
        o_ps = [ps(f"o_ps{n}", [P, 512]) for n in range(2)]
        i_ps = ps("i_ps", [P, 512])
        s_ps = ps("s_ps", [P, 512])

        loaded = sem("e_loaded")
        w_loaded = [sem(f"e_w_loaded{n}") for n in range(2)]
        table_ready = sem("table_ready")
        gathered = [sem(f"gathered{n}") for n in range(E)]
        weights_got = [sem(f"weights_got{n}") for n in range(E)]
        made = sem("e_made")
        zero_ready = sem("zero_ready")
        power_ready = sem("power_ready")
        stats_ready = sem("stats_ready")
        moments_ready = sem("moments_ready")
        var_ready = sem("e_var_ready")
        rstd_ready = sem("e_rstd_ready")
        normed_ready = sem("normed_ready")
        turned = sem("turned")
        xT_ready = sem("xT_ready")
        h_filled = sem("h_filled")
        h_read = sem("h_read")
        o_filled = sem("o_filled")
        weighted_ready = sem("weighted_ready")
        i_filled = sem("i_filled")
        same_ready = sem("same_ready")
        before_ready = sem("before_ready")
        dups_ready = sem("dups_ready")
        shift_ready = sem("shift_ready")
        target_ready = sem("target_ready")
        s_filled = sem("s_filled")
        summed_ready = sem("summed_ready")
        scattered = sem("scattered")
        copied = sem("copied")

        out_rows = d["out"].rearrange("b t c -> (b t) c")
        table = d["table"]
        weight_rows = d["combine_weights"]
        w1_dram = d["W1"].rearrange("e (c p) f -> e p c f", p=P)
        w2_dram = d["W2"].rearrange("e (n p) c -> e p n c", p=P)

        block = ctx.enter_context(nc.Block())

        @block.sync
        def _(sp):
            sp.dma_start(spare[:], d["spare"]).then_inc(loaded, 16)
            sp.dma_start(earlier[:], d["earlier"]).then_inc(loaded, 16)
            sp.dma_start(b1[:], d["b1"].rearrange("p (e n) -> p e n", e=E)).then_inc(loaded, 16)
            sp.dma_start(b2[:], d["b2"].rearrange("(a e) c -> a e c", a=1)).then_inc(loaded, 16)
            for e in range(E):
                if e >= 2:
                    sp.wait_ge(o_filled, TPE * (e - 1))
                sp.dma_start(w1[:, e % 2], w1_dram[e]).then_inc(w_loaded[e % 2], 16)
                sp.dma_start(w2[:, e % 2], w2_dram[e]).then_inc(w_loaded[e % 2], 16)
                if e == 0:
                    sp.wait_ge(gathered[0], 16 * TPE)
                    sp.dma_start(table[0:NTOK, :], out_rows[0:NTOK, :]).then_inc(table_ready, 16)
                    sp.wait_ge(zero_ready, 1)
                    sp.dma_start(table[NTOK:TABLE, :], zero[:]).then_inc(table_ready, 16)
            sp.wait_ge(scattered, 16 * NT)
            sp.dma_start(out_rows[0:NTOK, :], table[0:NTOK, :]).then_inc(copied, 16)
            sp.wait_ge(copied, 16)

        @block.gpsimd
        def _(pool):
            nc.gpsimd.memset(zero[:], 0.0).then_inc(zero_ready, 1)
            nc.gpsimd.memset(neg_half[:], -0.5).then_inc(power_ready, 1)
            pool.wait_ge(power_ready, 1)
            pool.wait_ge(ready, 16 * 3)

            def gather(t):
                at = bass.IndirectOffsetOnAxis(ap=idx[:, t:t + 1], axis=0)
                nc.gpsimd.indirect_dma_start(out=got[:, t, :], out_offset=None, in_=out_rows[:],
                                             in_offset=at).then_inc(gathered[t // TPE], 16)

            def gather_weights(t):
                at = bass.IndirectOffsetOnAxis(ap=idx[:, t:t + 1], axis=0)
                nc.gpsimd.indirect_dma_start(out=got_w[:, t, :], out_offset=None, in_=weight_rows[:],
                                             in_offset=at).then_inc(weights_got[t // TPE], 16)

            def root(e):
                if e >= E:
                    return
                ts = slice(e * TPE, (e + 1) * TPE)
                pool.wait_ge(var_ready, e + 1)
                nc.gpsimd.tensor_tensor(rstd[:, ts], rstd[:, ts], neg_half[:].to_broadcast([P, TPE]), ALU.pow) \
                    .then_inc(rstd_ready, 1)

            for e in range(AHEAD):
                for t in range(e * TPE, (e + 1) * TPE):
                    gather(t)
                for t in range(e * TPE, (e + 1) * TPE):
                    gather_weights(t)
                if e in (0, 2):
                    root(e // 2)
            pool.wait_ge(table_ready, 32)
            for t in range(NT):
                if t % TPE == 0:
                    root(t // TPE + 2)
                if t + AHEAD * TPE < NT:
                    gather(t + AHEAD * TPE)
                    gather_weights(t + AHEAD * TPE)
                pool.wait_ge(summed_ready, t + 1)
                pool.wait_ge(target_ready, t + 1)
                if t >= 1:
                    pool.wait_ge(scattered, 16 * t)
                nc.gpsimd.indirect_dma_start(
                    out=table[:], out_offset=bass.IndirectOffsetOnAxis(ap=target[:, t:t + 1], axis=0),
                    in_=summed[:, t % 2, :], in_offset=None, compute_op=ALU.add).then_inc(scattered, 16)

        @block.vector
        def _(dve):
            nc.vector.memset(ones_row[:], 1.0).then_inc(made, 1)
            dve.wait_ge(loaded, 16 * 4)
            dve.wait_ge(ready, 16 * 3)
            nc.vector.tensor_copy(idx_f[:], idx[:]).then_inc(made, 1)
            dve.wait_ge(made, 2)

            def statistics(e):
                dve.wait_ge(gathered[e], 16 * TPE)
                for t in range(e * TPE, (e + 1) * TPE):
                    nc.vector.bn_stats(stats[:, t, :], got[:, t, :]).then_inc(stats_ready, 1)
                for t in range(e * TPE, (e + 1) * TPE):
                    dve.wait_ge(stats_ready, t + 1)
                    nc.vector.bn_aggr(moments[:, t, :], stats[:, t, :]).then_inc(moments_ready, 1)
                dve.wait_ge(moments_ready, (e + 1) * TPE)
                ts = slice(e * TPE, (e + 1) * TPE)
                nc.vector.tensor_scalar(rstd[:, ts], moments[:, ts, 1], EPS, None, ALU.add).then_inc(var_ready, 1)

            def normalise(t):
                if t % TPE == 0:
                    dve.wait_ge(rstd_ready, t // TPE + 1)
                if t >= TPE:
                    dve.wait_ge(turned, t - TPE + 1)
                nc.vector.tensor_scalar(normed[:, t % TPE, :], got[:, t, :], moments[:, t, 0:1], rstd[:, t:t + 1],
                                        ALU.subtract, ALU.mult).then_inc(normed_ready, 1)

            def collect(t):
                if t >= 2:
                    dve.wait_ge(s_filled, t - 1)
                nc.vector.tensor_scalar(same[:, t % 2, :], i_ps[:, 0:P],
                                        idx_f[:, t:t + 1], None, ALU.is_equal).then_inc(same_ready, 1)

            def aim(t):
                dve.wait_ge(same_ready, t + 1)
                if t >= 1:
                    dve.wait_ge(dups_ready, t)
                nc.vector.tensor_tensor(same_before[:], same[:, t % 2, :], earlier[:], ALU.mult) \
                    .then_inc(before_ready, 1)
                nc.vector.tensor_scalar(shift_f[:, t:t + 1], idx_f[:, t:t + 1], spare[:, 0:1], -1.0, ALU.subtract,
                                        ALU.mult).then_inc(shift_ready, 1)
                dve.wait_ge(before_ready, t + 1)
                nc.vector.tensor_reduce(dups[:, t:t + 1], same_before[:], AX_X, ALU.max).then_inc(dups_ready, 1)
                dve.wait_ge(shift_ready, t + 1)
                dve.wait_ge(dups_ready, t + 1)
                nc.vector.scalar_tensor_tensor(target[:, t:t + 1], shift_f[:, t:t + 1], dups[:, t:t + 1],
                                               idx_f[:, t:t + 1], ALU.mult, ALU.add).then_inc(target_ready, 1)

            def take(t):
                dve.wait_ge(s_filled, t + 1)
                if t >= 2:
                    dve.wait_ge(scattered, 16 * (t - 1))
                nc.vector.tensor_copy(summed[:, t % 2, :], s_ps[:, 0:C]).then_inc(summed_ready, 1)

            statistics(0)
            for t in range(TPE):
                normalise(t)
            statistics(1)
            for e in range(E):
                if e + 1 < E:
                    for t in range((e + 1) * TPE, (e + 2) * TPE):
                        normalise(t)
                if e >= 1:
                    take(e * TPE - 1)
                if e + 2 < E:
                    statistics(e + 2)
                for j in range(TPE):
                    t = e * TPE + j
                    dve.wait_ge(i_filled, t + 1)
                    collect(t)
                    aim(t)
                    if j < TPE - 1:
                        take(t)
            take(NT - 1)

        @block.tensor
        def _(pe):
            pe.wait_ge(made, 2)

            def turn_index(t):
                nc.tensor.transpose(i_ps[:, 0:P], idx_f[:, t:t + 1].to_broadcast([P, P]),
                                    ident[:]).then_inc(i_filled, 1)

            def turn_rows(e):
                for j in range(TPE):
                    t = e * TPE + j
                    pe.wait_ge(normed_ready, t + 1)
                    if j == 0 and e >= 1:
                        pe.wait_ge(xT_ready, NC * e)
                    for c in range(NC):
                        last = nc.tensor.transpose(t_ps[c][:, j * P:(j + 1) * P], normed[:, t % TPE, c * P:(c + 1) * P],
                                                   ident[:])
                    last.then_inc(turned, 1)

            turn_rows(0)
            for e in range(E):
                pe.wait_ge(xT_ready, NC * (e + 1))
                pe.wait_ge(w_loaded[e % 2], 32 * (e // 2 + 1))
                for n in range(NF):
                    q = e * NF + n
                    if q >= 2:
                        pe.wait_ge(h_read, q - 1)
                    for c in range(NC):
                        last = nc.tensor.matmul(h_ps[q % 2][:], w1[:, e % 2, c, n * P:(n + 1) * P],
                                                xT[:, e % 2, c, :], start=(c == 0), stop=(c == NC - 1))
                    last.then_inc(h_filled, 1)
                if e >= 1:
                    sum_same(nc, pe, e * TPE - 1, same, weighted, s_ps, same_ready, weighted_ready, summed_ready, s_filled)
                if e + 1 < E:
                    turn_rows(e + 1)
                pe.wait_ge(h_read, NF * (e + 1))
                for j in range(TPE):
                    t = e * TPE + j
                    if t >= 2:
                        pe.wait_ge(weighted_ready, t - 1)
                    nc.tensor.matmul(o_ps[t % 2][:, 0:C], ones_row[:], b2[:, e, :], start=True, stop=False)
                    for n in range(NF):
                        last = nc.tensor.matmul(o_ps[t % 2][:, 0:C], hid[:, n, j * P:(j + 1) * P], w2[:, e % 2, n, :],
                                                start=False, stop=(n == NF - 1))
                    last.then_inc(o_filled, 1)
                    if t >= 1:
                        pe.wait_ge(same_ready, t)
                    turn_index(t)
                    if j >= 1:
                        sum_same(nc, pe, t - 1, same, weighted, s_ps, same_ready, weighted_ready, summed_ready, s_filled)
            sum_same(nc, pe, NT - 1, same, weighted, s_ps, same_ready, weighted_ready, summed_ready, s_filled)

        @block.scalar
        def _(act):
            def take_turned(e):
                act.wait_ge(turned, TPE * (e + 1))
                if e >= 2:
                    act.wait_ge(h_filled, NF * (e - 1))
                for c in range(NC):
                    nc.scalar.copy(xT[:, e % 2, c, :], t_ps[c][:]).then_inc(xT_ready, 1)

            act.wait_ge(loaded, 16 * 4)
            take_turned(0)
            for e in range(E):
                if e >= 1:
                    act.wait_ge(o_filled, TPE * e)
                for n in range(NF):
                    q = e * NF + n
                    act.wait_ge(h_filled, q + 1)
                    nc.scalar.activation(hid[:, n, :], h_ps[q % 2][:], ACT.Gelu_apprx_tanh,
                                         bias=b1[:, e, n:n + 1]).then_inc(h_read, 1)
                if e + 1 < E:
                    take_turned(e + 1)
                act.wait_ge(weights_got[e], 16 * TPE)
                for j in range(TPE):
                    t = e * TPE + j
                    act.wait_ge(o_filled, t + 1)
                    if t >= 2:
                        act.wait_ge(s_filled, t - 1)
                    nc.scalar.activation(weighted[:, t % 2, :], o_ps[t % 2][:, 0:C], ACT.Copy,
                                         scale=got_w[:, t, e:e + 1]).then_inc(weighted_ready, 1)


def sum_same(nc, pe, t, same, weighted, s_ps, same_ready, weighted_ready, summed_ready, s_filled):
    pe.wait_ge(same_ready, t + 1)
    pe.wait_ge(weighted_ready, t + 1)
    if t >= 1:
        pe.wait_ge(summed_ready, t)
    nc.tensor.matmul(s_ps[:, 0:C], same[:, t % 2, :], weighted[:, t % 2, :], start=True, stop=True) \
        .then_inc(s_filled, 1)


def build(nc, d):
    with ExitStack() as ctx:
        ident = ctx.enter_context(nc.sbuf_tensor("ident", [P, P], F32))
        params = ctx.enter_context(nc.sbuf_tensor("params", [P, NPAR], F32))
        idx = ctx.enter_context(nc.sbuf_tensor("idx", [P, NT], I32))
        ready = ctx.enter_context(nc.semaphore("w_ready"))
        with nc.Block() as block:
            @block.sync
            def _(sp):
                sp.dma_start(ident[:], d["ident"]).then_inc(ready, 16)
                sp.dma_start(params[:], d["params"]).then_inc(ready, 16)
                sp.dma_start(idx[:], d["idx"]).then_inc(ready, 16)
        attention_phase(nc, d, (ident, params, ready))
        expert_phase(nc, d, (ident, params, ready), idx)


def kernel(**inputs):
    import numpy as np
    import concourse.bacc as bacc
    from concourse.bass_utils import run_bass_kernel_spmd

    def get(name):
        return np.asarray(inputs[name])

    def columns(a):
        return a.reshape(-1, P).T

    attn = "L0_attn_"
    idx = get("L0_ffn_top_idx")
    if idx.dtype.itemsize == 8:
        idx = np.ascontiguousarray(idx).view(np.int32).reshape(CAP, E, 2)[:, :, 0]
    own = np.arange(P)
    arrays = {
        "x": get("x").reshape(B * T, 2, C).transpose(1, 2, 0),
        "tok_w": get("L0_tok_w"), "Wr": get(attn + "Wr"), "Wk": get(attn + "Wk"), "Wv": get(attn + "Wv"),
        "Wg": get(attn + "Wg"), "Wo": get(attn + "Wo"), "tm_w1": get(attn + "tm_w1"),
        "tm_w2": get(attn + "tm_w2").reshape(NMIX * LORA, C), "td_w1": get(attn + "td_w1"),
        "td_w2": get(attn + "td_w2"),
        "params": np.concatenate([columns(get(attn + n)) for n in
                                  ("time_maa_x", "time_maa_wkvrg", "time_decay", "time_faaaa", "ln_w", "ln_b")], 1),
        "ident": np.eye(P, dtype=np.float32),
        "head_block": (own[:, None] // K == own // K).astype(np.float32),
        "value_sum": ((own[:, None, None] // K == own // K)
                      & (own % K == np.arange(K)[:, None])).astype(np.float32).reshape(P, -1),
        "value_sel": ((own[:, None, None] // K == own // K)
                      & (own[:, None, None] % K == np.arange(K)[:, None])).astype(np.float32).reshape(P, -1),
        "idx": idx.reshape(TPE, P, E).transpose(1, 2, 0).reshape(P, NT),
        "spare": (NTOK + own[:, None]).astype(np.float32),
        "earlier": (own < own[:, None]).astype(np.float32),
        "b1": get("L0_ffn_b1").reshape(E, NF, P).transpose(2, 0, 1).reshape(P, E * NF),
        "b2": get("L0_ffn_b2"), "W1": get("L0_ffn_W1"), "W2": get("L0_ffn_W2"),
        "combine_weights": get("L0_ffn_combine_weights"),
    }
    arrays = {"in_" + name: np.ascontiguousarray(a) for name, a in arrays.items()}
    nc = bacc.Bacc("TRN2", target_bir_lowering=False, num_devices=1)
    d = {name[3:]: nc.dram_tensor(name, a.shape, mybir.dt.from_np(a.dtype), kind="ExternalInput").ap()
         for name, a in arrays.items()}
    d["out"] = nc.dram_tensor("out", (B, T, C), F32, kind="ExternalOutput").ap()
    d["table"] = nc.dram_tensor("table", (TABLE, C), F32, kind="Internal").ap()
    build(nc, d)
    r = run_bass_kernel_spmd(nc, [arrays], core_ids=[0])
    return r.results[0]["out"]
```
